# Optimizing a Trainium2 kernel written in Bass

```python
import numpy as np
import jax
import jax.numpy as jnp

def _softmax(x, axis=-1):
    return jax.nn.softmax(x, axis=axis)

def _gelu(x):
    return jax.nn.gelu(x, approximate=True)

def _silu(x):
    return jax.nn.silu(x)

def _sigmoid(x):
    return jax.nn.sigmoid(x)

def _layernorm(x, axis=-1, eps=1e-05):
    m = jnp.mean(x, axis=axis, keepdims=True)
    v = jnp.var(x, axis=axis, keepdims=True)
    return (x - m) / jnp.sqrt(v + eps)

def _scatter_add(tgt, idx, src, axis=0):
    return tgt.at[idx].add(src)

def _segment_sum(src, seg, n):
    return jax.ops.segment_sum(src, seg, n)
kernel_name = 'mk_flamingo_gated_d1_seqx_r4_f548e4'

def setup_inputs(seed: int=0):
    np.random.seed(seed)
    _w = jnp.asarray

    def _rec_inputs():
        import jax
        import jax.numpy as jnp
        _rk = jax.random.key(seed)
        x = -0.000125 + 0.9999 * jax.random.normal(jax.random.fold_in(_rk, 1), (8, 256, 1024), jnp.float32)
        _lenS = 256 - jax.random.randint(jax.random.fold_in(_rk, 7), (8,), 0, max(1, 256 // 4) + 1, jnp.int32)
        _lenS2 = 256 - jax.random.randint(jax.random.fold_in(_rk, 8), (8,), 0, max(1, 256 // 4) + 1, jnp.int32)
        _ctx_4096P = jax.random.normal(jax.random.fold_in(_rk, 11), (8, 16, 1024), jnp.float32)
        _ctx_4096c = jax.random.dirichlet(jax.random.fold_in(_rk, 511), 0.3 * jnp.ones((16,), jnp.float32), (8, 256))
        _ctx_4096t = jnp.einsum('bsk,bkd->bsd', _ctx_4096c, _ctx_4096P)
        _ctx_4096t = _ctx_4096t * jax.lax.rsqrt(jnp.mean(jnp.square(_ctx_4096t)) + 1e-12) * 0.953939
        ctx_4096 = -1.52775e-05 + 0.999936 * (_ctx_4096t + 0.3 * jax.random.normal(jax.random.fold_in(_rk, 611), (8, 256, 1024), jnp.float32))
        _g = jax.random.normal(jax.random.fold_in(_rk, 9001), (2, 1), jnp.float32)
        _g = jnp.sign(_g) * jnp.maximum(jnp.abs(_g), 1.0) + (_g == 0) * 1.0
        g_xattn = _g[0]
        g_ffn = _g[1]
        return (x, ctx_4096, g_xattn, g_ffn)
    x, ctx_4096, g_xattn, g_ffn = _rec_inputs()

    def _L0_xattn_setup():
        import jax, jax.numpy as jnp
        import numpy as np
        B, C, D = (8, 256, 1024)
        GROUPS = 8
        ATTN_SCALE = 1.0
        RESID = 1.0
        EPS = 1e-05
        key = jax.random.key(seed)
        ks = jax.random.split(key, 9)
        s = 1.0 / np.sqrt(C)
        return {'inp_q': jax.random.normal(ks[0], (B, C, D), jnp.float32), 'inp_k': jax.random.normal(ks[1], (B, C, D), jnp.float32), 'inp_v': jax.random.normal(ks[2], (B, C, D), jnp.float32), 'Wt': jax.random.normal(ks[3], (C, C), jnp.float32) * s, 'Wp': jax.random.normal(ks[4], (C, C), jnp.float32) * s, 'Wg': jax.random.normal(ks[5], (C, C), jnp.float32) * s, 'Wz': jax.random.normal(ks[6], (C, C // GROUPS), jnp.float32) * s, 'gn_w': jax.random.normal(ks[7], (C,), jnp.float32), 'gn_b': jax.random.normal(ks[8], (C,), jnp.float32)}
    _L0_xattn_all = _L0_xattn_setup()
    _L0_xattn_in = {k: v for k, v in _L0_xattn_all.items() if k in ('Wt', 'Wp', 'Wg', 'Wz', 'gn_w', 'gn_b')}
    del _L0_xattn_all

    def _L0_ffn_setup():
        import jax, jax.numpy as jnp
        import numpy as np
        D_IN = 1024
        D_OUT = 1024
        RANK = 16
        NUM_EXPERTS = 8
        TOP_K = 2
        SCALING = 32.0 / RANK
        key = jax.random.key(seed)
        ks = jax.random.split(key, 6)
        x = jax.random.normal(ks[0], (4, 512, D_IN), dtype=jnp.float32)
        W_base = jax.random.normal(ks[1], (D_OUT, D_IN), dtype=jnp.float32) * (1.0 / np.sqrt(D_IN))
        b_base = jax.random.normal(ks[2], (D_OUT,), dtype=jnp.float32) * 0.01
        W_router = jax.random.normal(ks[3], (NUM_EXPERTS, D_IN), dtype=jnp.float32) * 0.01
        A_stack = jax.random.uniform(ks[4], (NUM_EXPERTS, RANK, D_IN), dtype=jnp.float32, minval=-1.0, maxval=1.0) * (1.0 / np.sqrt(D_IN))
        B_stack = jax.random.normal(ks[5], (NUM_EXPERTS, D_OUT, RANK), dtype=jnp.float32) * 0.02
        return {'x': x, 'W_base': W_base, 'b_base': b_base, 'W_router': W_router, 'A_stack': A_stack, 'B_stack': B_stack}
    _L0_ffn_all = _L0_ffn_setup()
    _L0_ffn_in = {k: v for k, v in _L0_ffn_all.items() if k in ('W_base', 'b_base', 'W_router', 'A_stack', 'B_stack')}
    del _L0_ffn_all
    return {'x': x, 'ctx_4096': ctx_4096, 'g_xattn': g_xattn, 'g_ffn': g_ffn, 'L0_xattn_Wt': _L0_xattn_in['Wt'], 'L0_xattn_Wp': _L0_xattn_in['Wp'], 'L0_xattn_Wg': _L0_xattn_in['Wg'], 'L0_xattn_Wz': _L0_xattn_in['Wz'], 'L0_xattn_gn_w': _L0_xattn_in['gn_w'], 'L0_xattn_gn_b': _L0_xattn_in['gn_b'], 'L0_ffn_W_base': _L0_ffn_in['W_base'], 'L0_ffn_b_base': _L0_ffn_in['b_base'], 'L0_ffn_W_router': _L0_ffn_in['W_router'], 'L0_ffn_A_stack': _L0_ffn_in['A_stack'], 'L0_ffn_B_stack': _L0_ffn_in['B_stack']}

def reference(x, ctx_4096, g_xattn, g_ffn, L0_xattn_Wt, L0_xattn_Wp, L0_xattn_Wg, L0_xattn_Wz, L0_xattn_gn_w, L0_xattn_gn_b, L0_ffn_W_base, L0_ffn_b_base, L0_ffn_W_router, L0_ffn_A_stack, L0_ffn_B_stack):
    import jax
    import jax.numpy as jnp

    def _L0_xattn_ref(inp_q, inp_k, inp_v, Wt, Wp, Wg, Wz, gn_w, gn_b):
        import jax, jax.numpy as jnp
        import numpy as np
        B, C, D = (8, 256, 1024)
        GROUPS = 8
        ATTN_SCALE = 1.0
        RESID = 1.0
        EPS = 1e-05
        residual = inp_v * RESID
        t = jnp.einsum('oc,bcd->bod', Wt, inp_v)
        p = jnp.einsum('oc,bcd->bod', Wp, inp_q)
        g = jnp.einsum('oc,bcd->bod', Wg, inp_k)
        b, c, d = t.shape
        cg = c // GROUPS
        tg = t.reshape(b, GROUPS, cg * d)
        pg = p.reshape(b, GROUPS, cg * d)
        gg = g.reshape(b, GROUPS, cg * d)
        att = jnp.sum(pg * gg, axis=-1, keepdims=True) * ATTN_SCALE
        x = (att * tg).reshape(b, c, d)
        xg = x.reshape(b, GROUPS, cg, d)
        Wzg = Wz.reshape(GROUPS, cg, cg)
        y = jnp.einsum('goi,bgid->bgod', Wzg, xg).reshape(b, c, d)
        yg = y.reshape(b, GROUPS, cg * d)
        mu = jnp.mean(yg, axis=-1, keepdims=True)
        var = jnp.var(yg, axis=-1, keepdims=True)
        yn = ((yg - mu) * jax.lax.rsqrt(var + EPS)).reshape(b, c, d)
        return yn * gn_w[None, :, None] + gn_b[None, :, None] + residual

    def _L0_ffn_ref(x, W_base, b_base, W_router, A_stack, B_stack):
        import jax, jax.numpy as jnp
        import numpy as np
        D_IN = 1024
        D_OUT = 1024
        RANK = 16
        NUM_EXPERTS = 8
        TOP_K = 2
        SCALING = 32.0 / RANK
        orig_shape = x.shape
        xf = x.reshape(-1, D_IN)
        logits = xf @ W_router.T
        probs = jax.nn.softmax(logits, axis=-1)
        topk_p, topk_i = jax.lax.top_k(probs, TOP_K)
        topk_p = topk_p / jnp.sum(topk_p, axis=-1, keepdims=True)
        combine = jnp.sum(jax.nn.one_hot(topk_i, NUM_EXPERTS, dtype=xf.dtype) * topk_p[..., None], axis=1)
        h = jnp.einsum('nd,erd->ner', xf, A_stack)
        h = h * combine[..., None]
        lora_out = jnp.einsum('ner,eor->no', h, B_stack) * SCALING
        base_out = xf @ W_base.T + b_base
        out = base_out + lora_out
        return out.reshape(orig_shape[:-1] + (D_OUT,))
    x = x + jnp.tanh(g_xattn[0]) * _L0_xattn_ref(_layernorm(x, axis=-1), ctx_4096, ctx_4096, L0_xattn_Wt, L0_xattn_Wp, L0_xattn_Wg, L0_xattn_Wz, L0_xattn_gn_w, L0_xattn_gn_b)
    x = x + jnp.tanh(g_ffn[0]) * _L0_ffn_ref(_layernorm(x, axis=-1), L0_ffn_W_base, L0_ffn_b_base, L0_ffn_W_router, L0_ffn_A_stack, L0_ffn_B_stack)
    return x

_drawn_inputs = setup_inputs


def setup_inputs(seed=0):
    import zlib

    import numpy as np

    out = dict(_drawn_inputs(seed))
    spreads = {}
    factors = {'L0_ffn_b_base': 8.0}
    for name, (base, spread) in spreads.items():
        noise = np.random.default_rng([zlib.crc32(name.encode()), seed]).standard_normal(out[name].shape)
        drawn = base * np.exp(spread * noise) if base else spread * noise
        out[name] = jnp.asarray(drawn.astype(out[name].dtype))
    for name, factor in factors.items():
        out[name] = (out[name] * factor).astype(out[name].dtype)
    return out
```

```python
from contextlib import ExitStack

import concourse.bass as bass
from concourse import mybir

ALU = mybir.AluOpType
ACT = mybir.ActivationFunctionType
AX = mybir.AxisListType
F32 = mybir.dt.float32
F32R = mybir.dt.float32r

P = 128
EPS = 1e-5
TOP_K = 2
TINY = 1.2e-38


def gated_block_kernel(nc, x, ctx, g_xattn, g_ffn, wt, wp_t, wg_t, wz_t, gn_cols,
                       w_ext_t, b_base, b_stack_t, out):
    NB, C, D = x.shape
    T = C // P
    GROUPS, CG = wz_t.shape[0], wz_t.shape[1]
    NF = 512
    HALVES = D // NF
    PAIRS = T * HALVES
    KD = D // P
    WEXT = w_ext_t.shape[1]
    ER = b_stack_t.shape[0]
    E = WEXT - ER - D
    R = ER // E
    LORA_SCALE = 32.0 / R
    BASE = ER + E
    CHUNKS = [(0, BASE + 256), (BASE + 256, BASE + 640), (BASE + 640, WEXT)]
    NQ = 2 * T
    QB = KD // 2
    SPLITS = KD + 1
    PARTS = ((0, 0), (1, 0), (0, 1))
    assert T == 2 and HALVES == 2 and CG == 32 and ER == P and KD == 8

    x_v = x.rearrange("b (t p) d -> b p t d", p=P)
    ctx_v = ctx.rearrange("b (t p) d -> b p t d", p=P)
    out_v = out.rearrange("b (t p) d -> b p t d", p=P)

    with ExitStack() as stack:
        def sb(name, shape, dt=F32):
            return stack.enter_context(nc.sbuf_tensor(name, shape, dt))

        def sem(name):
            return stack.enter_context(nc.semaphore(name))

        def split(name, shape):
            return [sb(name + "_hi", shape, F32R), sb(name + "_lo", shape, F32R)]

        w_ext = split("w_ext", [P, KD, WEXT])
        b_up = split("b_up", [P, D])
        w_m = split("w_m", [P, T, C])
        w_p = split("w_p", [P, T, C])
        w_g = split("w_g", [P, T, C])
        tf_bias = sb("tf_bias", [P, D])
        x_raw = sb("x_raw", [P, T, D])
        ctx_raw = sb("ctx_raw", [P, T, D])
        xn = sb("xn", [P, D])
        g_sb = xn[:, :].rearrange("p (s n) -> p s n", s=2)
        xs = split("xs", [P, T, D])
        cs = split("cs", [P, T, D])
        w_sum = sb("w_sum", [P, T, D])
        y0 = sb("y0", [P, T, D])
        x1 = sb("x1", [P, T, D])
        xt = split("xt", [P, KD, C])
        late = sb("late", [P, T * D + D])
        resid = late[:, 0:T * D].rearrange("p (t d) -> p t d", t=T)
        fin = late[:, T * D:T * D + D]
        stage = [late[:, s * WEXT:(s + 1) * WEXT] for s in range(2)]
        hc = sb("hc", [P, T, ER])
        hct = split("hct", [P, T, P])
        raw = x1[:, :, :].rearrange("p t d -> p (t d)")
        wt_raw = raw[:, 0:T * C].rearrange("p (t c) -> p t c", t=T)
        wp_raw = raw[:, T * C:2 * T * C].rearrange("p (t c) -> p t c", t=T)
        wg_raw = raw[:, 2 * T * C:3 * T * C].rearrange("p (t c) -> p t c", t=T)
        wz_raw = raw[:, 3 * T * C:3 * T * C + T * P].rearrange("p (t c) -> p t c", t=T)
        ident = sb("ident", [P, P])
        group_ones = sb("group_ones", [P, P])
        tie = sb("tie", [P, E, E])
        minus_half = sb("minus_half", [P, T])
        gates = sb("gates", [P, 2])
        tg = sb("tg", [P, 2])
        gn_wb = sb("gn_wb", [P, 2, T])
        gn_tg = sb("gn_tg", [P, 2, T])
        carrier = sb("carrier", [P, 2])
        x_stats = sb("x_stats", [P, T, HALVES, 6])
        x_mv = sb("x_mv", [P, T, 2])
        x_var = sb("x_var", [P, T])
        x_rstd = sb("x_rstd", [P, T])
        y_stats = sb("y_stats", [P, T, HALVES, 6])
        row_sums = sb("row_sums", [P, T, 4])
        att = sb("att", [P, T])
        g_mean = sb("g_mean", [P, T])
        dev = sb("dev", [P, T])
        dev2 = sb("dev2", [P, T])
        row_var = sb("row_var", [P, T])
        att2 = sb("att2", [P, T])
        att_w = sb("att_w", [P, T])
        g_var = sb("g_var", [P, T])
        g_var_eps = sb("g_var_eps", [P, T])
        g_rstd = sb("g_rstd", [P, T])
        gn_scale = sb("gn_scale", [P, T])
        gn_drop = sb("gn_drop", [P, T])
        gn_shift = sb("gn_shift", [P, T])
        x1_stats = sb("x1_stats", [P, T, HALVES, 6])
        x1_mv = sb("x1_mv", [P, T, 2])
        x1_neg_mean = sb("x1_neg_mean", [P, T])
        x1_var = sb("x1_var", [P, T])
        x1_rstd = sb("x1_rstd", [P, T])
        fin_scale = sb("fin_scale", [P, T])
        fin_shift = sb("fin_shift", [P, T])
        logit = sb("logit", [P, T, E])
        neg_max = sb("neg_max", [P, T])
        prob = sb("prob", [P, T, E])
        diff = sb("diff", [P, T, E, E])
        beats = sb("beats", [P, T, E, E])
        rank = sb("rank", [P, T, E])
        top = sb("top", [P, T, E])
        top_sum = sb("top_sum", [P, T])
        top_inv = sb("top_inv", [P, T])
        combine = sb("combine", [P, T, E])

        bank = [stack.enter_context(nc.psum_tensor(f"bank{n}", [P, NF], F32)) for n in range(8)]
        tr_bank = [bank[0], bank[1]]
        first_bank = [bank[2], bank[3]]
        p_bank, g_bank = [bank[4], bank[6]], [bank[5], bank[7]]
        y_bank = [bank[4], bank[5], bank[6], bank[7]]
        rest_bank = [[bank[4], bank[5]], [bank[6], bank[7]]]

        small_loaded = sem("small_loaded")
        gn_loaded = sem("gn_loaded")
        wz_cleared = sem("wz_cleared")
        attn_w_loaded = sem("attn_w_loaded")
        bias_loaded = sem("bias_loaded")
        stage_loaded = [sem("stage0_loaded"), sem("stage1_loaded")]
        tanh_done = sem("tanh_done")
        consts_ready = sem("consts_ready")
        consts_filled = sem("consts_filled")
        ident_zeroed = sem("ident_zeroed")
        ident_ready = sem("ident_ready")
        m_done = sem("m_done")
        attn_w_hi = sem("attn_w_hi")
        attn_w_ready = sem("attn_w_ready")
        w_hi_ready = sem("w_hi_ready")
        w_lo_ready = sem("w_lo_ready")
        gn_tg_ready = sem("gn_tg_ready")
        tf_bias_ready = sem("tf_bias_ready")
        x_loaded = sem("x_loaded")
        ctx_loaded = sem("ctx_loaded")
        x_var_ready = sem("x_var_ready")
        x_rstd_ready = sem("x_rstd_ready")
        xn_ready = sem("xn_ready")
        x_hi_ready = sem("x_hi_ready")
        x_lo_ready = sem("x_lo_ready")
        c_hi_ready = sem("c_hi_ready")
        c_lo_ready = sem("c_lo_ready")
        w_sum_ready = sem("w_sum_ready")
        p_done = sem("p_done")
        g_done = sem("g_done")
        g_copied = sem("g_copied")
        att_part = sem("att_part")
        y_done = sem("y_done")
        y_copied = sem("y_copied")
        means_ready = sem("means_ready")
        means_summed = sem("means_summed")
        vars_ready = sem("vars_ready")
        vars_summed = sem("vars_summed")
        g_var_ready = sem("g_var_ready")
        g_rstd_ready = sem("g_rstd_ready")
        x1_ready = sem("x1_ready")
        x1_var_ready = sem("x1_var_ready")
        x1_rstd_ready = sem("x1_rstd_ready")
        x1c_ready = sem("x1c_ready")
        resid_ready = sem("resid_ready")
        xt_done = sem("xt_done")
        xt_hi_ready = sem("xt_hi_ready")
        xt_lo_ready = sem("xt_lo_ready")
        first_done = sem("first_done")
        fin_scalars_ready = sem("fin_scalars_ready")
        gate_in_ready = sem("gate_in_ready")
        exp_done = sem("exp_done")
        hc_ready = sem("hc_ready")
        hct_done = sem("hct_done")
        hct_hi_ready = sem("hct_hi_ready")
        hct_lo_ready = sem("hct_lo_ready")
        ffn_done = sem("ffn_done")
        banks_read = sem("banks_read")
        added = sem("added")
        stored = sem("stored")
        CREDIT = 2 * T
        x_chain = sem("x_chain")
        y_chain = sem("y_chain")
        gn_chain = sem("gn_chain")
        x1_chain = sem("x1_chain")
        gate_chain = sem("gate_chain")

        def count(per_batch, b, k):
            return per_batch * b + k

        def credited(per_batch, b, k):
            return 1 + count(per_batch, b, k)

        def banks_read_by(b, t):
            return CREDIT + T * b + t + 1

        block = stack.enter_context(nc.Block())

        @block.sync
        def _(sp):
            def load(b):
                sp.wait_ge(w_sum_ready, count(T, b, 0))
                sp.dma_start(x_raw[:, :, :], x_v[b]).then_inc(x_loaded, 16)
                sp.wait_ge(c_lo_ready, count(T, b, 0))
                sp.dma_start(ctx_raw[:, :, :], ctx_v[b]).then_inc(ctx_loaded, 16)

            def store(b):
                for t in range(T):
                    sp.wait_ge(added, credited(T, b, t + 1))
                    sp.dma_start(out_v[b][:, t, :], fin).then_inc(stored, 16)

            load(0)
            sp.dma_start(gates[:, 0:1], g_xattn.partition_broadcast(P)).then_inc(small_loaded, 16)
            sp.dma_start(gates[:, 1:2], g_ffn.partition_broadcast(P)).then_inc(small_loaded, 16)
            for dst, src in ((wt_raw, wt), (wp_raw, wp_t), (wg_raw, wg_t)):
                sp.dma_start(dst, src.rearrange("(t p) c -> p t c", p=P)).then_inc(attn_w_loaded, 16)
            sp.wait_ge(wz_cleared, 1)
            for q in range(P // CG):
                sp.dma_start(wz_raw[q * CG:(q + 1) * CG, :, q * CG:(q + 1) * CG],
                             wz_t.rearrange("(t q) i o -> q i t o", t=T)[q]).then_inc(attn_w_loaded, 16)
            sp.dma_start(gn_wb[:, :, :], gn_cols).then_inc(gn_loaded, 16)
            sp.dma_start(tf_bias[:, :], b_base.partition_broadcast(P)).then_inc(bias_loaded, 16)
            for n in range(2):
                sp.dma_start(stage[n], w_ext_t[n * P:(n + 1) * P, :]).then_inc(stage_loaded[n], 16)
            load(1)
            for n in range(2, SPLITS):
                sp.wait_ge(w_lo_ready, n - 1)
                src = w_ext_t[n * P:(n + 1) * P, :] if n < KD else b_stack_t
                sp.dma_start(stage[n % 2][:, 0:src.shape[1]], src).then_inc(stage_loaded[n % 2], 16)
            with sp.Fori(1, NB - 1) as i:
                load(i + 1)
                store(i - 1)
            store(NB - 2)
            store(NB - 1)
            sp.wait_ge(stored, credited(16 * T, NB, 0))

        @block.gpsimd
        def _(pool):
            def rstd_x(b):
                pool.wait_ge(x_var_ready, count(1, b, 1))
                nc.gpsimd.tensor_tensor(x_rstd[:, :], x_var[:, :], minus_half[:, :], ALU.pow)\
                    .then_inc(x_rstd_ready, 1)

            def ctx_low(b):
                for t in range(T):
                    pool.wait_ge(c_hi_ready, count(T, b, t + 1))
                    nc.gpsimd.tensor_tensor(cs[1][:, t, :], ctx_raw[:, t, :], cs[0][:, t, :].bitcast(F32),
                                            ALU.subtract).then_inc(c_lo_ready, 1)

            def rstd_group(b):
                pool.wait_ge(g_var_ready, count(1, b, 1))
                nc.gpsimd.tensor_tensor(g_rstd[:, :], g_var_eps[:, :], minus_half[:, :], ALU.pow)\
                    .then_inc(g_rstd_ready, 1)

            def rstd_x1(b):
                pool.wait_ge(x1_var_ready, count(1, b, 1))
                nc.gpsimd.tensor_tensor(x1_rstd[:, :], x1_var[:, :], minus_half[:, :], ALU.pow)\
                    .then_inc(x1_rstd_ready, 1)

            def residual(b):
                pool.wait_ge(added, credited(T, b, 0))
                for t in range(T):
                    pool.wait_ge(x1_ready, count(T, b, t + 1))
                    nc.gpsimd.tensor_tensor(resid[:, t, :], x1[:, t, :], tf_bias[:, :], ALU.add)\
                        .then_inc(resid_ready, 1)

            def add(b, t):
                pool.wait_ge(resid_ready, count(T, b, t + 1))
                pool.wait_ge(banks_read, banks_read_by(b, t))
                nc.gpsimd.tensor_tensor(fin, fin, resid[:, t, :], ALU.add).then_inc(added, 1)

            nc.gpsimd.memset(ident[:, :], 0.0).then_inc(ident_zeroed, 1)
            pool.wait_ge(ident_zeroed, 1)
            nc.gpsimd.affine_select(out=ident[:, :], in_=ident[:, :], compare_op=ALU.not_equal, fill=1.0,
                                    base=0, pattern=[[-1, P]], channel_multiplier=1).then_inc(ident_ready, 1)
            pool.wait_ge(consts_ready, 1)
            rstd_x(0)
            ctx_low(0)
            for n in range(SPLITS):
                if n == 3:
                    rstd_x(1)
                pool.wait_ge(w_hi_ready, n + 1)
                hi, lo = (w_ext[0][:, n, :], w_ext[1][:, n, :]) if n < KD else (b_up[0][:, :], b_up[1][:, :])
                nc.gpsimd.tensor_tensor(lo, stage[n % 2][:, 0:lo.shape[1]], hi.bitcast(F32), ALU.subtract)\
                    .then_inc(w_lo_ready, 1)
            ctx_low(1)
            rstd_group(0)
            rstd_x1(0)
            pool.wait_ge(w_lo_ready, SPLITS)
            pool.wait_ge(tf_bias_ready, 1)

            def step(i, prepare):
                residual(i - 1)
                if prepare:
                    rstd_x(i + 1)
                    ctx_low(i + 1)
                rstd_group(i)
                add(i - 1, 0)
                rstd_x1(i)
                add(i - 1, 1)

            with pool.Fori(1, NB - 1) as i:
                step(i, True)
            step(NB - 1, False)
            residual(NB - 1)
            add(NB - 1, 0)
            add(NB - 1, 1)

        @block.scalar
        def _(act):
            def ctx_high(b, t):
                if t == 0:
                    act.wait_ge(ctx_loaded, count(16, b, 16))
                    act.wait_ge(y_done, count(PAIRS, b, 0))
                nc.scalar.activation(cs[0][:, t, :], ctx_raw[:, t, :], ACT.Copy).then_inc(c_hi_ready, 1)

            def x_high(b, t):
                act.wait_ge(xn_ready, count(T, b, t + 1))
                act.wait_ge(p_done, count(PAIRS, b, 0))
                nc.scalar.activation(xs[0][:, t, :], xn[:, :], ACT.Copy).then_inc(x_hi_ready, 1)

            def g_copy(b, n):
                act.wait_ge(g_done, count(PAIRS, b, n + 1))
                if n >= 2:
                    act.wait_ge(att_part, count(PAIRS, b, n - 1))
                nc.scalar.activation(g_sb[:, n % 2, :], g_bank[n % 2][:, :], ACT.Copy).then_inc(g_copied, 1)

            def y_copy(b, n):
                act.wait_ge(y_done, count(PAIRS, b, n + 1))
                m, h = n // HALVES, n % HALVES
                nc.scalar.activation(y0[:, m, h * NF:(h + 1) * NF], y_bank[n][:, :], ACT.Copy)\
                    .then_inc(y_copied, 1)

            def x1_center(b):
                act.wait_ge(x1_var_ready, count(1, b, 1))
                for t in range(T):
                    nc.scalar.activation(y0[:, t, :], x1[:, t, :], ACT.Identity, bias=x1_neg_mean[:, t:t + 1])\
                        .then_inc(x1c_ready, 1)

            def xt_high(b, q):
                t, h = q // 2, q % 2
                act.wait_ge(xt_done, count(NQ, b, q + 1))
                nc.scalar.activation(xt[0][:, h * QB:(h + 1) * QB, t * P:(t + 1) * P],
                                     tr_bank[q % 2][:, :].rearrange("p (k n) -> p k n", k=QB), ACT.Copy)\
                    .then_inc(xt_hi_ready, 1)

            def exps(b, t):
                act.wait_ge(gate_in_ready, count(T, b, t + 1))
                nc.scalar.activation(prob[:, t, :], logit[:, t, :], ACT.Exp, bias=neg_max[:, t:t + 1])\
                    .then_inc(exp_done, 1)

            def hct_high(b, t):
                act.wait_ge(hct_done, count(T, b, t + 1))
                nc.scalar.activation(hct[0][:, t, :], tr_bank[1][:, 0:P], ACT.Copy).then_inc(hct_hi_ready, 1)

            def finish(b, t):
                act.wait_ge(fin_scalars_ready, count(1, b, 1))
                act.wait_ge(stored, credited(16 * T, b, 16 * t))
                act.wait_ge(ffn_done, count(T, b, t + 1))
                banks = [first_bank[t][:, BASE:CHUNKS[0][1]]]
                banks += [rest_bank[t][n][:, 0:CHUNKS[n + 1][1] - CHUNKS[n + 1][0]] for n in range(2)]
                for (lo, hi), src in zip(CHUNKS, banks):
                    last = nc.scalar.activation(fin[:, max(lo - BASE, 0):hi - BASE], src, ACT.Identity,
                                                bias=fin_shift[:, t:t + 1], scale=fin_scale[:, t:t + 1])
                last.then_inc(banks_read, 1)

            act.wait_ge(small_loaded, 32)
            nc.scalar.activation(tg[:, :], gates[:, :], ACT.Tanh).then_inc(tanh_done, 1)
            act.wait_ge(attn_w_loaded, 16 * (3 + P // CG))
            nc.scalar.activation(w_p[0][:, :, :], wp_raw, ACT.Copy).then_inc(attn_w_hi, 1)
            nc.scalar.activation(w_g[0][:, :, :], wg_raw, ACT.Copy).then_inc(attn_w_hi, 1)
            act.wait_ge(m_done, 1)
            nc.scalar.activation(w_m[0][:, :, :], bank[0][:, :].rearrange("p (t c) -> p t c", t=T), ACT.Copy)\
                .then_inc(attn_w_hi, 1)
            ctx_high(0, 0)
            ctx_high(0, 1)
            x_high(0, 0)
            x_high(0, 1)

            def stage_high(n):
                act.wait_ge(stage_loaded[n % 2], 16 * (n // 2 + 1))
                hi = w_ext[0][:, n, :] if n < KD else b_up[0][:, :]
                nc.scalar.activation(hi, stage[n % 2][:, 0:hi.shape[1]], ACT.Copy).then_inc(w_hi_ready, 1)

            act.sem_inc(banks_read, CREDIT)
            for free in (hct_lo_ready, added, stored):
                act.sem_inc(free, 1)
            stage_high(0)
            stage_high(1)
            for n in range(PAIRS):
                g_copy(0, n)
                stage_high(n + 2)
            for n in range(PAIRS):
                y_copy(0, n)
                if n == 1:
                    x_high(1, 0)
            ctx_high(1, 0)
            ctx_high(1, 1)
            for n in range(PAIRS + 2, SPLITS):
                stage_high(n)
            x_high(1, 1)
            x1_center(0)

            def step(i, prepare):
                for n in range(PAIRS):
                    g_copy(i, n)
                for q in range(NQ):
                    xt_high(i - 1, q)
                for n in range(PAIRS):
                    y_copy(i, n)
                    if n == 1 and prepare:
                        x_high(i + 1, 0)
                if prepare:
                    ctx_high(i + 1, 0)
                    ctx_high(i + 1, 1)
                    x_high(i + 1, 1)
                exps(i - 1, 0)
                exps(i - 1, 1)
                hct_high(i - 1, 0)
                finish(i - 1, 0)
                x1_center(i)
                hct_high(i - 1, 1)
                finish(i - 1, 1)

            with act.Fori(1, NB - 1) as i:
                step(i, True)
            step(NB - 1, False)
            for q in range(NQ):
                xt_high(NB - 1, q)
            exps(NB - 1, 0)
            exps(NB - 1, 1)
            hct_high(NB - 1, 0)
            finish(NB - 1, 0)
            hct_high(NB - 1, 1)
            finish(NB - 1, 1)

        @block.vector
        def _(dve):
            def x_stat(b, t):
                if t == 0:
                    dve.wait_ge(x_loaded, count(16, b, 16))
                for h in range(HALVES):
                    last = nc.vector.bn_stats(x_stats[:, t, h, :], x_raw[:, t, h * NF:(h + 1) * NF])
                if t == T - 1:
                    last.then_inc(x_chain, 1)

            def x_scalars(b):
                dve.wait_ge(x_chain, count(2, b, 1))
                nc.vector.memset(carrier[:, :], 0.0)
                for t in range(T):
                    last = nc.vector.bn_aggr(x_mv[:, t, :], x_stats[:, t, :, :])
                last.then_inc(x_chain, 1)
                dve.wait_ge(x_chain, count(2, b, 2))
                nc.vector.tensor_scalar(x_var[:, :], x_mv[:, :, 1], EPS, None, ALU.add).then_inc(x_var_ready, 1)

            def x_norm(b, t):
                if t == 0:
                    dve.wait_ge(x_rstd_ready, count(1, b, 1))
                    dve.wait_ge(att_part, count(PAIRS, b, 0))
                dve.wait_ge(x_lo_ready, count(T, b, t))
                nc.vector.tensor_scalar(xn[:, :], x_raw[:, t, :], x_mv[:, t, 0:1], x_rstd[:, t:t + 1],
                                        ALU.subtract, ALU.mult).then_inc(xn_ready, 1)

            def x_low(b, t):
                dve.wait_ge(x_hi_ready, count(T, b, t + 1))
                nc.vector.tensor_tensor(xs[1][:, t, :], xn[:, :], xs[0][:, t, :].bitcast(F32), ALU.subtract)\
                    .then_inc(x_lo_ready, 1)

            def sum_inputs(b):
                dve.wait_ge(ctx_loaded, count(16, b, 16))
                for t in range(T):
                    nc.vector.scalar_tensor_tensor(w_sum[:, t, :], ctx_raw[:, t, :], tg[:, 0:1], x_raw[:, t, :],
                                                   ALU.mult, ALU.add).then_inc(w_sum_ready, 1)

            def att_sum(b, n):
                m, h = n // HALVES, n % HALVES
                dve.wait_ge(p_done, count(PAIRS, b, n + 1))
                dve.wait_ge(g_copied, count(PAIRS, b, n + 1))
                g = g_sb[:, n % 2, :]
                nc.vector.tensor_tensor_reduce(g, p_bank[n % 2][:, :], g, 1.0, 0.0, ALU.mult, ALU.add,
                                               row_sums[:, m, h:h + 1]).then_inc(att_part, 1)

            def y_stat(b):
                for n in range(PAIRS):
                    m, h = n // HALVES, n % HALVES
                    dve.wait_ge(y_copied, count(PAIRS, b, n + 1))
                    last = nc.vector.bn_stats(y_stats[:, m, h, :], y0[:, m, h * NF:(h + 1) * NF])
                last.then_inc(y_chain, 1)
                dve.wait_ge(y_chain, count(1, b, 1))
                nc.vector.memset(carrier[:, :], 0.0)
                for m in range(T):
                    last = nc.vector.bn_aggr(row_sums[:, m, 2:4], y_stats[:, m, :, :])
                last.then_inc(means_ready, 1)

            def group_means(b):
                def link(ins, k):
                    ins.then_inc(gn_chain, 1)
                    dve.wait_ge(gn_chain, count(6, b, k))
                sums = bank[0][:, 0:3 * T].rearrange("p (t k) -> p t k", t=T)
                dve.wait_ge(means_summed, count(1, b, 1))
                nc.vector.tensor_reduce(att[:, :], sums[:, :, 0:2], AX.X, ALU.add)
                link(nc.vector.tensor_scalar(g_mean[:, :], sums[:, :, 2], 1.0 / CG, None, ALU.mult), 1)
                nc.vector.tensor_tensor(att2[:, :], att[:, :], att[:, :], ALU.mult)
                link(nc.vector.tensor_tensor(dev[:, :], row_sums[:, :, 2], g_mean[:, :], ALU.subtract), 2)
                nc.vector.tensor_tensor(att_w[:, :], att[:, :], gn_tg[:, 0, :], ALU.mult)
                link(nc.vector.tensor_tensor(dev2[:, :], dev[:, :], dev[:, :], ALU.mult), 3)
                nc.vector.tensor_tensor(row_var[:, :], dev2[:, :], row_sums[:, :, 3], ALU.add)\
                    .then_inc(vars_ready, 1)

            def group_scalars(b):
                def link(ins, k):
                    ins.then_inc(gn_chain, 1)
                    dve.wait_ge(gn_chain, count(6, b, k))
                dve.wait_ge(vars_summed, count(1, b, 1))
                link(nc.vector.scalar_tensor_tensor(g_var[:, :], bank[0][:, 0:T], 1.0 / CG, att2[:, :],
                                                    ALU.mult, ALU.mult), 4)
                nc.vector.tensor_scalar(g_var_eps[:, :], g_var[:, :], EPS, None, ALU.add)\
                    .then_inc(g_var_ready, 1)
                dve.wait_ge(g_rstd_ready, count(1, b, 1))
                link(nc.vector.tensor_tensor(gn_scale[:, :], att_w[:, :], g_rstd[:, :], ALU.mult), 5)
                link(nc.vector.tensor_tensor(gn_drop[:, :], gn_scale[:, :], g_mean[:, :], ALU.mult), 6)
                nc.vector.tensor_tensor(gn_shift[:, :], gn_tg[:, 1, :], gn_drop[:, :], ALU.subtract)

            def x1_sum(b):
                dve.wait_ge(w_sum_ready, count(T, b, T))
                dve.wait_ge(x1c_ready, count(T, b, 0))
                dve.wait_ge(resid_ready, count(T, b, 0))
                for t in range(T):
                    nc.vector.scalar_tensor_tensor(x1[:, t, :], y0[:, t, :], gn_scale[:, t:t + 1],
                                                   w_sum[:, t, :], ALU.mult, ALU.add).then_inc(x1_ready, 1)

            def x1_stat(b):
                for t in range(T):
                    dve.wait_ge(x1_ready, count(T, b, t + 1))
                    for h in range(HALVES):
                        last = nc.vector.bn_stats(x1_stats[:, t, h, :], x1[:, t, h * NF:(h + 1) * NF])
                last.then_inc(x1_chain, 1)
                dve.wait_ge(x1_chain, count(2, b, 1))
                nc.vector.memset(carrier[:, :], 0.0)
                for t in range(T):
                    last = nc.vector.bn_aggr(x1_mv[:, t, :], x1_stats[:, t, :, :])
                last.then_inc(x1_chain, 1)
                dve.wait_ge(x1_chain, count(2, b, 2))
                nc.vector.tensor_scalar(x1_neg_mean[:, :], x1_mv[:, :, 0], -1.0, None, ALU.mult)
                nc.vector.tensor_scalar(x1_var[:, :], x1_mv[:, :, 1], EPS, None, ALU.add)\
                    .then_inc(x1_var_ready, 1)

            def xt_low(b, q):
                t, h = q // 2, q % 2
                at = (slice(None), slice(h * QB, (h + 1) * QB), slice(t * P, (t + 1) * P))
                dve.wait_ge(xt_hi_ready, count(NQ, b, q + 1))
                nc.vector.tensor_tensor(xt[1][at], tr_bank[q % 2][:, :].rearrange("p (k n) -> p k n", k=QB),
                                        xt[0][at].bitcast(F32), ALU.subtract).then_inc(xt_lo_ready, 1)

            def fin_scalars(b):
                dve.wait_ge(x1_rstd_ready, count(1, b, 1))
                dve.wait_ge(banks_read, banks_read_by(b - 1, T - 1))
                nc.vector.tensor_scalar(fin_scale[:, :], x1_rstd[:, :], tg[:, 1:2], None, ALU.mult)
                nc.vector.tensor_copy(fin_shift[:, :], gn_shift[:, :]).then_inc(fin_scalars_ready, 1)

            def gate(b, t):
                def link(ins, k):
                    ins.then_inc(gate_chain, 1)
                    dve.wait_ge(gate_chain, count(7 * T, b, 7 * t + k))
                dve.wait_ge(first_done, count(T, b, t + 1))
                link(nc.vector.tensor_scalar(logit[:, t, :], first_bank[t][:, ER:BASE], x1_rstd[:, t:t + 1],
                                             None, ALU.mult), 1)
                nc.vector.tensor_reduce(neg_max[:, t:t + 1], logit[:, t, :], AX.X, ALU.max, negate=True)\
                    .then_inc(gate_in_ready, 1)
                link(nc.vector.tensor_tensor(diff[:, t, :, :],
                                             logit[:, t, :].unsqueeze(1).broadcast_to((P, E, E)),
                                             logit[:, t, :].unsqueeze(2).broadcast_to((P, E, E)),
                                             ALU.subtract), 2)
                link(nc.vector.tensor_tensor(beats[:, t, :, :], diff[:, t, :, :], tie[:, :, :], ALU.is_ge), 3)
                link(nc.vector.tensor_reduce(rank[:, t, :], beats[:, t, :, :], AX.X, ALU.add), 4)
                dve.wait_ge(exp_done, count(T, b, t + 1))
                link(nc.vector.scalar_tensor_tensor(top[:, t, :], rank[:, t, :], TOP_K - 0.5, prob[:, t, :],
                                                    ALU.is_lt, ALU.mult, accum_out=top_sum[:, t:t + 1]), 5)
                link(nc.vector.reciprocal(top_inv[:, t:t + 1], top_sum[:, t:t + 1]), 6)
                link(nc.vector.tensor_scalar(combine[:, t, :], top[:, t, :], top_inv[:, t:t + 1], LORA_SCALE,
                                             ALU.mult, ALU.mult), 7)
                nc.vector.tensor_tensor(hc[:, t, :].rearrange("p (e r) -> p e r", e=E),
                                        first_bank[t][:, 0:ER].rearrange("p (e r) -> p e r", e=E),
                                        combine[:, t, :].unsqueeze(2).broadcast_to((P, E, R)),
                                        ALU.mult).then_inc(hc_ready, 1)

            def hct_low(b, t):
                dve.wait_ge(hct_hi_ready, count(T, b, t + 1))
                nc.vector.tensor_tensor(hct[1][:, t, :], tr_bank[1][:, 0:P], hct[0][:, t, :].bitcast(F32),
                                        ALU.subtract).then_inc(hct_lo_ready, 1)

            nc.vector.memset(wz_raw, 0.0).then_inc(wz_cleared, 1)
            nc.vector.memset(group_ones[:, :], 0.0)
            nc.vector.memset(tie[:, :, :], TINY).then_inc(consts_filled, 1)
            nc.vector.memset(minus_half[:, :], -0.5).then_inc(consts_ready, 1)
            x_stat(0, 0)
            x_stat(0, 1)
            x_scalars(0)
            dve.wait_ge(consts_filled, 1)
            for q in range(P // CG):
                nc.vector.memset(group_ones[q * CG:(q + 1) * CG, q * CG:(q + 1) * CG], 1.0)
            for e in range(1, E):
                nc.vector.memset(tie[:, e, 0:e], 0.0)
            x_norm(0, 0)
            dve.wait_ge(attn_w_hi, 2)
            for parts, whole in ((w_p, wp_raw), (w_g, wg_raw)):
                nc.vector.tensor_tensor(parts[1][:, :, :], whole, parts[0][:, :, :].bitcast(F32), ALU.subtract)
            dve.wait_ge(attn_w_hi, 3)
            nc.vector.tensor_tensor(w_m[1][:, :, :], bank[0][:, :].rearrange("p (t c) -> p t c", t=T),
                                    w_m[0][:, :, :].bitcast(F32), ALU.subtract).then_inc(attn_w_ready, 1)
            x_low(0, 0)
            x_norm(0, 1)
            x_low(0, 1)
            dve.wait_ge(tanh_done, 1)
            sum_inputs(0)
            dve.wait_ge(gn_loaded, 16)
            nc.vector.tensor_scalar(gn_tg[:, :, :], gn_wb[:, :, :], tg[:, 0:1], None, ALU.mult)\
                .then_inc(gn_tg_ready, 1)
            dve.wait_ge(gn_tg_ready, 1)
            for n in range(PAIRS):
                att_sum(0, n)
                if n == 1:
                    x_stat(1, 0)
                if n == 2:
                    x_stat(1, 1)
                    x_scalars(1)
            dve.wait_ge(bias_loaded, 16)
            nc.vector.tensor_scalar(tf_bias[:, :], tf_bias[:, :], tg[:, 1:2], None, ALU.mult)\
                .then_inc(tf_bias_ready, 1)
            x_norm(1, 0)
            y_stat(0)
            x_low(1, 0)
            x_norm(1, 1)
            group_means(0)
            x_low(1, 1)
            group_scalars(0)
            x1_sum(0)
            x1_stat(0)
            sum_inputs(1)

            def step(i, prepare):
                for n in range(PAIRS):
                    att_sum(i, n)
                    if prepare and n == 1:
                        x_stat(i + 1, 0)
                    if prepare and n == 2:
                        x_stat(i + 1, 1)
                        x_scalars(i + 1)
                for q in range(NQ):
                    xt_low(i - 1, q)
                if prepare:
                    x_norm(i + 1, 0)
                y_stat(i)
                if prepare:
                    x_low(i + 1, 0)
                    x_norm(i + 1, 1)
                fin_scalars(i - 1)
                gate(i - 1, 0)
                if prepare:
                    x_low(i + 1, 1)
                gate(i - 1, 1)
                group_means(i)
                hct_low(i - 1, 0)
                group_scalars(i)
                x1_sum(i)
                x1_stat(i)
                hct_low(i - 1, 1)
                if prepare:
                    sum_inputs(i + 1)

            with dve.Fori(1, NB - 1) as i:
                step(i, True)
            step(NB - 1, False)
            for q in range(NQ):
                xt_low(NB - 1, q)
            fin_scalars(NB - 1)
            gate(NB - 1, 0)
            gate(NB - 1, 1)
            hct_low(NB - 1, 0)
            hct_low(NB - 1, 1)

        @block.tensor
        def _(pe):
            def product(dst, weights, w_at, moving, m_at, steps):
                for k in range(steps):
                    for a, c in PARTS:
                        last = nc.tensor.matmul(dst, w_at(weights[a], k), m_at(moving[c], k),
                                                start=(k == 0 and (a, c) == PARTS[0]),
                                                stop=(k == steps - 1 and (a, c) == PARTS[-1]))
                return last

            def chunk(weights, moving, dst, n):
                m, h = n // HALVES, n % HALVES
                return product(dst, weights, lambda w, k: w[:, k, m * P:(m + 1) * P],
                               moving, lambda v, k: v[:, k, h * NF:(h + 1) * NF], T)

            def pairs(b):
                pe.wait_ge(x_lo_ready, count(T, b, T))
                for n in range(PAIRS):
                    if n < 2:
                        pe.wait_ge(banks_read, banks_read_by(b - 2, n))
                    else:
                        pe.wait_ge(att_part, count(PAIRS, b, n - 1))
                    chunk(w_p, xs, p_bank[n % 2][:, :], n).then_inc(p_done, 1)
                    if n == 0:
                        pe.wait_ge(c_lo_ready, count(T, b, T))
                    chunk(w_g, cs, g_bank[n % 2][:, :], n).then_inc(g_done, 1)

            def transposes(b):
                for q in range(NQ):
                    t, h = q // 2, q % 2
                    if h == 0:
                        pe.wait_ge(x1c_ready, count(T, b, t + 1))
                    if q == 0:
                        pe.wait_ge(g_var_ready, count(1, b, 1))
                    elif q == 1:
                        pe.wait_ge(hct_lo_ready, credited(T, b, 0))
                    else:
                        pe.wait_ge(xt_lo_ready, count(NQ, b, q - 1))
                    for j in range(QB):
                        k = h * QB + j
                        last = nc.tensor.transpose(tr_bank[q % 2][:, j * P:(j + 1) * P],
                                                   y0[:, t, k * P:(k + 1) * P], ident[:, :])
                    last.then_inc(xt_done, 1)

            def y_products(b):
                for n in range(PAIRS):
                    pe.wait_ge(att_part, count(PAIRS, b, 3 + n // 2))
                    chunk(w_m, cs, y_bank[n][:, :], n).then_inc(y_done, 1)

            def ffn_chunk(b, t, dst, n):
                lo, hi = CHUNKS[n]
                return product(dst, xt, lambda w, k: w[:, k, t * P:(t + 1) * P],
                               w_ext, lambda v, k: v[:, k, lo:hi], KD)

            def first_chunk(b, t):
                pe.wait_ge(xt_lo_ready, count(NQ, b, 2 * t + 2))
                pe.wait_ge(banks_read, banks_read_by(b - 1, t))
                if t == 0:
                    pe.wait_ge(w_lo_ready, SPLITS)
                ffn_chunk(b, t, first_bank[t][:, 0:CHUNKS[0][1]], 0).then_inc(first_done, 1)

            def sum_means(b, ffn):
                pe.wait_ge(means_ready, count(1, b, 1))
                if ffn:
                    pe.wait_ge(xt_lo_ready, count(NQ, b - 1, 3))
                nc.tensor.matmul(bank[0][:, 0:3 * T].rearrange("p (t k) -> p t k", t=T), group_ones[:, :],
                                 row_sums[:, :, 0:3], start=True, stop=True).then_inc(means_summed, 1)

            def sum_vars(b):
                pe.wait_ge(vars_ready, count(1, b, 1))
                nc.tensor.matmul(bank[0][:, 0:T], group_ones[:, :], row_var[:, :], start=True, stop=True)\
                    .then_inc(vars_summed, 1)

            def rest(b, t, beside, ffn_attention):
                width = [hi - lo for lo, hi in CHUNKS]
                for n in range(2):
                    if ffn_attention:
                        pe.wait_ge(y_copied, count(PAIRS, b + 1, 2 * t + n + 1))
                    ffn_chunk(b, t, rest_bank[t][n][:, 0:width[n + 1]], n + 1)
                    if n == 0:
                        pe.wait_ge(hc_ready, count(T, b, t + 1))
                        if t == 0:
                            pe.wait_ge(xt_lo_ready, count(NQ, b, NQ))
                        else:
                            pe.wait_ge(hct_lo_ready, credited(T, b, t))
                        nc.tensor.transpose(tr_bank[1][:, 0:P], hc[:, t, :], ident[:, :]).then_inc(hct_done, 1)
                        beside()
                pe.wait_ge(hct_lo_ready, credited(T, b, t + 1))
                dsts = [first_bank[t][:, BASE:width[0]], rest_bank[t][0][:, 0:width[1]],
                        rest_bank[t][1][:, 0:width[2]]]
                for (lo, hi), dst in zip(CHUNKS, dsts):
                    for a, c in PARTS:
                        last = nc.tensor.matmul(dst, hct[a][:, t, :], b_up[c][:, max(lo - BASE, 0):hi - BASE],
                                                start=False, stop=True, skip_group_check=True)
                last.then_inc(ffn_done, 1)

            pe.wait_ge(attn_w_loaded, 16 * (3 + P // CG))
            for m in range(T):
                for k in range(T):
                    last = nc.tensor.matmul(bank[0][:, m * C + k * P:m * C + (k + 1) * P],
                                            wt_raw[:, k, m * P:(m + 1) * P], wz_raw[:, k, :],
                                            start=True, stop=True)
            last.then_inc(m_done, 1)
            pe.wait_ge(attn_w_ready, 1)
            pairs(0)
            y_products(0)
            sum_means(0, False)
            sum_vars(0)
            pe.wait_ge(ident_ready, 1)

            with pe.Fori(1, NB) as i:
                pairs(i)
                transposes(i - 1)
                y_products(i)
                first_chunk(i - 1, 0)
                first_chunk(i - 1, 1)
                sum_means(i, True)
                rest(i - 1, 0, lambda: sum_vars(i), True)
                rest(i - 1, 1, lambda: None, True)
            transposes(NB - 1)
            first_chunk(NB - 1, 0)
            first_chunk(NB - 1, 1)
            rest(NB - 1, 0, lambda: None, False)
            rest(NB - 1, 1, lambda: None, False)


_OUT_SHAPE = (8, 256, 1024)


def kernel(x, ctx_4096, g_xattn, g_ffn, L0_xattn_Wt, L0_xattn_Wp, L0_xattn_Wg, L0_xattn_Wz, L0_xattn_gn_w,
           L0_xattn_gn_b, L0_ffn_W_base, L0_ffn_b_base, L0_ffn_W_router, L0_ffn_A_stack, L0_ffn_B_stack):
    import numpy as np
    import concourse.bacc as bacc
    from concourse.bass_utils import run_bass_kernel_spmd

    groups = 8
    cg = L0_xattn_Wz.shape[1]
    experts, rank, d = L0_ffn_A_stack.shape
    a_rows = np.asarray(L0_ffn_A_stack).reshape(experts * rank, d)
    w_rows = np.concatenate([a_rows, np.asarray(L0_ffn_W_router), np.asarray(L0_ffn_W_base)], axis=0)
    arrays = {
        "x": x, "ctx": ctx_4096, "g_xattn": g_xattn, "g_ffn": g_ffn,
        "wt": L0_xattn_Wt, "wp_t": np.asarray(L0_xattn_Wp).T, "wg_t": np.asarray(L0_xattn_Wg).T,
        "wz_t": np.asarray(L0_xattn_Wz).reshape(groups, cg, cg).transpose(0, 2, 1),
        "gn_cols": np.stack([L0_xattn_gn_w, L0_xattn_gn_b]).reshape(2, -1, P).transpose(2, 0, 1),
        "w_ext_t": w_rows.T, "b_base": L0_ffn_b_base,
        "b_stack_t": np.asarray(L0_ffn_B_stack).transpose(0, 2, 1).reshape(experts * rank, -1),
    }
    nc = bacc.Bacc("TRN2", target_bir_lowering=False, num_devices=1)
    feeds, args = {}, []
    for name, a in arrays.items():
        a = np.ascontiguousarray(a)
        feeds[f"in_{name}"] = a
        args.append(nc.dram_tensor(f"in_{name}", a.shape, mybir.dt.from_np(a.dtype), kind="ExternalInput").ap())
    out = nc.dram_tensor("out", _OUT_SHAPE, F32, kind="ExternalOutput").ap()
    gated_block_kernel(nc, *args, out)
    r = run_bass_kernel_spmd(nc, [feeds], core_ids=[0])
    return r.results[0]["out"]
```

```python
from contextlib import ExitStack

import concourse.bass as bass
from concourse import mybir

ALU = mybir.AluOpType
ACT = mybir.ActivationFunctionType
AX = mybir.AxisListType
F32 = mybir.dt.float32
F32R = mybir.dt.float32r

P = 128
EPS = 1e-5
TOP_K = 2
TINY = 1.2e-38


def gated_block_kernel(nc, x, ctx, g_both, wt, wp_t, wg_t, wz_t, gn_cols,
                       w_ext_t, b_base, b_stack_t, out):
    NB, C, D = x.shape
    T = C // P
    GROUPS, CG = wz_t.shape[0], wz_t.shape[1]
    NF = 512
    HALVES = D // NF
    PAIRS = T * HALVES
    KD = D // P
    WEXT = w_ext_t.shape[1]
    ER = b_stack_t.shape[0]
    E = WEXT - ER - D
    R = ER // E
    LORA_SCALE = 32.0 / R
    BASE = ER + E
    CHUNKS = [(0, BASE + 256), (BASE + 256, BASE + 640), (BASE + 640, WEXT)]
    NQ = 2 * T
    QB = KD // 2
    SPLITS = KD + 1
    PARTS = ((0, 0), (1, 0), (0, 1))
    assert T == 2 and HALVES == 2 and CG == 32 and ER == P and KD == 8

    x_v = x.rearrange("b (t p) d -> b p t d", p=P)
    ctx_v = ctx.rearrange("b (t p) d -> b p t d", p=P)
    out_v = out.rearrange("b (t p) d -> b p t d", p=P)

    with ExitStack() as stack:
        def sb(name, shape, dt=F32):
            return stack.enter_context(nc.sbuf_tensor(name, shape, dt))

        def sem(name):
            return stack.enter_context(nc.semaphore(name))

        def split(name, shape):
            return [sb(name + "_hi", shape, F32R), sb(name + "_lo", shape, F32R)]

        w_ext = split("w_ext", [P, KD, WEXT])
        b_up = split("b_up", [P, D])
        w_m = split("w_m", [P, T, C])
        w_p = split("w_p", [P, T, C])
        w_g = split("w_g", [P, T, C])
        tf_bias = sb("tf_bias", [P, D])
        x_raw = sb("x_raw", [P, T, D])
        ctx_raw = sb("ctx_raw", [P, T, D])
        xn = sb("xn", [P, D])
        g_sb = xn[:, :].rearrange("p (s n) -> p s n", s=2)
        xs = split("xs", [P, T, D])
        cs = split("cs", [P, T, D])
        w_sum = sb("w_sum", [P, T, D])
        y0 = sb("y0", [P, T, D])
        x1 = sb("x1", [P, T, D])
        xt = split("xt", [P, KD, C])
        late = sb("late", [P, T * D + D])
        resid = late[:, 0:T * D].rearrange("p (t d) -> p t d", t=T)
        fin = late[:, T * D:T * D + D]
        hc = sb("hc", [P, T, ER])
        hct = split("hct", [P, T, P])
        raw = x1[:, :, :].rearrange("p t d -> p (t d)")
        wt_raw = raw[:, 0:T * C].rearrange("p (t c) -> p t c", t=T)
        wp_raw = raw[:, T * C:2 * T * C].rearrange("p (t c) -> p t c", t=T)
        wg_raw = raw[:, 2 * T * C:3 * T * C].rearrange("p (t c) -> p t c", t=T)
        wz_raw = raw[:, 3 * T * C:3 * T * C + T * P].rearrange("p (t c) -> p t c", t=T)
        stage = [late[:, 0:WEXT], late[:, WEXT:2 * WEXT], raw[:, 0:WEXT]]
        NSTAGE = len(stage)
        assert SPLITS % NSTAGE == 0
        ident = sb("ident", [P, P])
        group_ones = sb("group_ones", [P, P])
        tie = sb("tie", [P, E, E])
        minus_half = sb("minus_half", [P, T])
        gates = sb("gates", [P, 2])
        tg = sb("tg", [P, 2])
        gn_wb = sb("gn_wb", [P, 2, T])
        gn_tg = sb("gn_tg", [P, 2, T])
        carrier = sb("carrier", [P, 2])
        x_stats = sb("x_stats", [P, T, HALVES, 6])
        x_mv = sb("x_mv", [P, T, 2])
        x_var = sb("x_var", [P, T])
        x_rstd = sb("x_rstd", [P, T])
        y_stats = sb("y_stats", [P, T, HALVES, 6])
        row_sums = sb("row_sums", [P, T, 4])
        att = sb("att", [P, T])
        g_mean = sb("g_mean", [P, T])
        dev = sb("dev", [P, T])
        dev2 = sb("dev2", [P, T])
        row_var = sb("row_var", [P, T])
        att2 = sb("att2", [P, T])
        att_w = sb("att_w", [P, T])
        g_var = sb("g_var", [P, T])
        g_var_eps = sb("g_var_eps", [P, T])
        g_rstd = sb("g_rstd", [P, T])
        gn_scale = sb("gn_scale", [P, T])
        gn_drop = sb("gn_drop", [P, T])
        gn_shift = sb("gn_shift", [P, T])
        x1_stats = sb("x1_stats", [P, T, HALVES, 6])
        x1_mv = sb("x1_mv", [P, T, 2])
        x1_neg_mean = sb("x1_neg_mean", [P, T])
        x1_var = sb("x1_var", [P, T])
        x1_rstd = sb("x1_rstd", [P, T])
        fin_scale = sb("fin_scale", [P, T])
        fin_shift = sb("fin_shift", [P, T])
        logit = sb("logit", [P, T, E])
        neg_max = sb("neg_max", [P, T])
        prob = sb("prob", [P, T, E])
        diff = sb("diff", [P, T, E, E])
        beats = sb("beats", [P, T, E, E])
        rank = sb("rank", [P, T, E])
        top = sb("top", [P, T, E])
        top_sum = sb("top_sum", [P, T])
        top_inv = sb("top_inv", [P, T])
        combine = sb("combine", [P, T, E])

        bank = [stack.enter_context(nc.psum_tensor(f"bank{n}", [P, NF], F32)) for n in range(8)]
        tr_bank = [bank[0], bank[1]]
        first_bank = [bank[2], bank[3]]
        p_bank, g_bank = [bank[4], bank[6]], [bank[5], bank[7]]
        y_bank = [bank[4], bank[5], bank[6], bank[7]]
        rest_bank = [[bank[4], bank[5]], [bank[6], bank[7]]]

        small_loaded = sem("small_loaded")
        gn_loaded = sem("gn_loaded")
        wz_cleared = sem("wz_cleared")
        wp_wg_loaded = sem("wp_wg_loaded")
        wt_wz_loaded = sem("wt_wz_loaded")
        bias_loaded = sem("bias_loaded")
        stage_loaded = [sem(f"stage{n}_loaded") for n in range(NSTAGE)]
        stage_split = [sem(f"stage{n}_split") for n in range(NSTAGE)]
        tanh_done = sem("tanh_done")
        consts_ready = sem("consts_ready")
        consts_filled = sem("consts_filled")
        ident_zeroed = sem("ident_zeroed")
        ident_ready = sem("ident_ready")
        m_done = sem("m_done")
        wp_wg_hi = sem("wp_wg_hi")
        wp_wg_ready = sem("wp_wg_ready")
        wm_hi = sem("wm_hi")
        wm_ready = sem("wm_ready")
        w_hi_ready = sem("w_hi_ready")
        gn_tg_ready = sem("gn_tg_ready")
        tf_bias_ready = sem("tf_bias_ready")
        x_loaded = [sem(f"x{t}_loaded") for t in range(T)]
        ctx_loaded = sem("ctx_loaded")
        x_var_ready = sem("x_var_ready")
        x_rstd_ready = sem("x_rstd_ready")
        xn_ready = sem("xn_ready")
        x_hi_ready = sem("x_hi_ready")
        x_lo_ready = sem("x_lo_ready")
        c_hi_ready = sem("c_hi_ready")
        c_lo_ready = sem("c_lo_ready")
        w_sum_ready = sem("w_sum_ready")
        p_done = sem("p_done")
        g_done = sem("g_done")
        g_copied = sem("g_copied")
        att_part = sem("att_part")
        y_done = sem("y_done")
        y_copied = sem("y_copied")
        means_ready = sem("means_ready")
        means_summed = sem("means_summed")
        vars_ready = sem("vars_ready")
        vars_summed = sem("vars_summed")
        g_var_ready = sem("g_var_ready")
        g_rstd_ready = sem("g_rstd_ready")
        x1_ready = sem("x1_ready")
        x1_var_ready = sem("x1_var_ready")
        x1_rstd_ready = sem("x1_rstd_ready")
        x1c_ready = sem("x1c_ready")
        resid_ready = sem("resid_ready")
        xt_done = sem("xt_done")
        xt_hi_ready = sem("xt_hi_ready")
        xt_lo_ready = sem("xt_lo_ready")
        first_done = sem("first_done")
        fin_scalars_ready = sem("fin_scalars_ready")
        gate_in_ready = sem("gate_in_ready")
        exp_done = sem("exp_done")
        hc_ready = sem("hc_ready")
        hct_done = sem("hct_done")
        hct_hi_ready = sem("hct_hi_ready")
        hct_lo_ready = sem("hct_lo_ready")
        ffn_done = sem("ffn_done")
        banks_read = sem("banks_read")
        added = sem("added")
        stored = sem("stored")
        CREDIT = 2 * T
        x_chain = sem("x_chain")
        y_chain = sem("y_chain")
        gn_chain = sem("gn_chain")
        x1_chain = sem("x1_chain")
        gate_chain = sem("gate_chain")

        def count(per_batch, b, k):
            return per_batch * b + k

        def credited(per_batch, b, k):
            return 1 + count(per_batch, b, k)

        def banks_read_by(b, t):
            return CREDIT + T * b + t + 1

        def stage_parts(n):
            return [w[:, n, :] for w in w_ext] if n < KD else [w[:, :] for w in b_up]

        block = stack.enter_context(nc.Block())

        @block.sync
        def _(sp):
            def load(b):
                sp.wait_ge(w_sum_ready, count(T, b, 0))
                for t in range(T):
                    sp.dma_start(x_raw[:, t, :], x_v[b][:, t, :]).then_inc(x_loaded[t], 16)
                sp.wait_ge(c_lo_ready, count(T, b, 0))
                sp.dma_start(ctx_raw[:, :, :], ctx_v[b]).then_inc(ctx_loaded, 16)

            def store(b, t):
                sp.wait_ge(added, credited(T, b, t + 1))
                sp.dma_start(out_v[b][:, t, :], fin).then_inc(stored, 16)

            def load_stage(n):
                if n >= NSTAGE:
                    sp.wait_ge(stage_split[n % NSTAGE], n // NSTAGE)
                elif n == NSTAGE - 1:
                    sp.wait_ge(wp_wg_ready, 1)
                    sp.wait_ge(m_done, 1)
                src = w_ext_t[n * P:(n + 1) * P, :] if n < KD else b_stack_t
                sp.dma_start(stage[n % NSTAGE][:, 0:src.shape[1]], src).then_inc(stage_loaded[n % NSTAGE], 16)

            load(0)
            sp.dma_start(gn_wb[:, :, :], gn_cols).then_inc(gn_loaded, 16)
            load_stage(0)
            load_stage(1)
            load_stage(2)
            sp.dma_start(tf_bias[:, :], b_base.partition_broadcast(P)).then_inc(bias_loaded, 16)
            load_stage(3)
            load(1)
            for n in range(4, SPLITS):
                load_stage(n)
            load(2)
            with sp.Fori(1, NB - 2) as i:
                store(i - 1, 0)
                load(i + 2)
                store(i - 1, 1)
            for b in range(NB - 3, NB):
                for t in range(T):
                    store(b, t)
            sp.wait_ge(stored, credited(16 * T, NB, 0))

        @block.gpsimd
        def _(pool):
            def rstd_x(b):
                pool.wait_ge(x_var_ready, count(1, b, 1))
                nc.gpsimd.tensor_tensor(x_rstd[:, :], x_var[:, :], minus_half[:, :], ALU.pow)\
                    .then_inc(x_rstd_ready, 1)

            def ctx_low(b, t):
                pool.wait_ge(c_hi_ready, count(T, b, t + 1))
                nc.gpsimd.tensor_tensor(cs[1][:, t, :], ctx_raw[:, t, :], cs[0][:, t, :].bitcast(F32),
                                        ALU.subtract).then_inc(c_lo_ready, 1)

            def rstd_group(b):
                pool.wait_ge(g_var_ready, count(1, b, 1))
                nc.gpsimd.tensor_tensor(g_rstd[:, :], g_var_eps[:, :], minus_half[:, :], ALU.pow)\
                    .then_inc(g_rstd_ready, 1)

            def rstd_x1(b):
                pool.wait_ge(x1_var_ready, count(1, b, 1))
                nc.gpsimd.tensor_tensor(x1_rstd[:, :], x1_var[:, :], minus_half[:, :], ALU.pow)\
                    .then_inc(x1_rstd_ready, 1)

            def residual(b):
                pool.wait_ge(added, credited(T, b, 0))
                for t in range(T):
                    pool.wait_ge(x1_ready, count(T, b, t + 1))
                    nc.gpsimd.tensor_tensor(resid[:, t, :], x1[:, t, :], tf_bias[:, :], ALU.add)\
                        .then_inc(resid_ready, 1)

            def add(b, t):
                pool.wait_ge(resid_ready, count(T, b, t + 1))
                pool.wait_ge(banks_read, banks_read_by(b, t))
                nc.gpsimd.tensor_tensor(fin, fin, resid[:, t, :], ALU.add).then_inc(added, 1)

            nc.gpsimd.memset(ident[:, :], 0.0).then_inc(ident_zeroed, 1)
            pool.wait_ge(ident_zeroed, 1)
            nc.gpsimd.affine_select(out=ident[:, :], in_=ident[:, :], compare_op=ALU.not_equal, fill=1.0,
                                    base=0, pattern=[[-1, P]], channel_multiplier=1).then_inc(ident_ready, 1)
            def stage_low(n):
                pool.wait_ge(w_hi_ready, n + 1)
                hi, lo = stage_parts(n)
                nc.gpsimd.tensor_tensor(lo, stage[n % NSTAGE][:, 0:lo.shape[1]], hi.bitcast(F32), ALU.subtract)\
                    .then_inc(stage_split[n % NSTAGE], 1)

            pool.wait_ge(consts_ready, 1)
            rstd_x(0)
            ctx_low(0, 1)
            stage_low(0)
            stage_low(1)
            stage_low(3)
            rstd_x(1)
            stage_low(4)
            stage_low(6)
            ctx_low(1, 1)
            rstd_group(0)
            stage_low(7)
            rstd_x1(0)
            for n in range(2):
                pool.wait_ge(stage_split[n], SPLITS // NSTAGE)
            pool.wait_ge(tf_bias_ready, 1)

            def step(i, prepare):
                residual(i - 1)
                if prepare:
                    rstd_x(i + 1)
                    ctx_low(i + 1, 0)
                    ctx_low(i + 1, 1)
                rstd_group(i)
                add(i - 1, 0)
                rstd_x1(i)
                add(i - 1, 1)

            with pool.Fori(1, NB - 1) as i:
                step(i, True)
            step(NB - 1, False)
            residual(NB - 1)
            add(NB - 1, 0)
            add(NB - 1, 1)

        @block.scalar
        def _(act):
            def ctx_high(b, t):
                if t == 0:
                    act.wait_ge(ctx_loaded, count(16, b, 16))
                    act.wait_ge(y_done, count(PAIRS, b, 0))
                nc.scalar.activation(cs[0][:, t, :], ctx_raw[:, t, :], ACT.Copy).then_inc(c_hi_ready, 1)

            def x_high(b, t, normed):
                act.wait_ge(xn_ready, count(T, b, t + 1))
                act.wait_ge(p_done, count(PAIRS, b, 0))
                nc.scalar.activation(xs[0][:, t, :], normed, ACT.Copy).then_inc(x_hi_ready, 1)

            def g_copy(b, n):
                act.wait_ge(g_done, count(PAIRS, b, n + 1))
                if n >= 2:
                    act.wait_ge(att_part, count(PAIRS, b, n - 1))
                nc.scalar.activation(g_sb[:, n % 2, :], g_bank[n % 2][:, :], ACT.Copy).then_inc(g_copied, 1)

            def y_copy(b, n):
                act.wait_ge(y_done, count(PAIRS, b, n + 1))
                m, h = n // HALVES, n % HALVES
                nc.scalar.activation(y0[:, m, h * NF:(h + 1) * NF], y_bank[n][:, :], ACT.Copy)\
                    .then_inc(y_copied, 1)

            def x1_center(b):
                act.wait_ge(x1_var_ready, count(1, b, 1))
                for t in range(T):
                    nc.scalar.activation(y0[:, t, :], x1[:, t, :], ACT.Identity, bias=x1_neg_mean[:, t:t + 1])\
                        .then_inc(x1c_ready, 1)

            def xt_high(b, q):
                t, h = q // 2, q % 2
                act.wait_ge(xt_done, count(NQ, b, q + 1))
                nc.scalar.activation(xt[0][:, h * QB:(h + 1) * QB, t * P:(t + 1) * P],
                                     tr_bank[q % 2][:, :].rearrange("p (k n) -> p k n", k=QB), ACT.Copy)\
                    .then_inc(xt_hi_ready, 1)

            def exps(b, t):
                act.wait_ge(gate_in_ready, count(T, b, t + 1))
                nc.scalar.activation(prob[:, t, :], logit[:, t, :], ACT.Exp, bias=neg_max[:, t:t + 1])\
                    .then_inc(exp_done, 1)

            def hct_high(b, t):
                act.wait_ge(hct_done, count(T, b, t + 1))
                nc.scalar.activation(hct[0][:, t, :], tr_bank[1][:, 0:P], ACT.Copy).then_inc(hct_hi_ready, 1)

            def finish(b, t):
                act.wait_ge(fin_scalars_ready, count(1, b, 1))
                act.wait_ge(stored, credited(16 * T, b, 16 * t))
                act.wait_ge(ffn_done, count(T, b, t + 1))
                banks = [first_bank[t][:, BASE:CHUNKS[0][1]]]
                banks += [rest_bank[t][n][:, 0:CHUNKS[n + 1][1] - CHUNKS[n + 1][0]] for n in range(2)]
                for (lo, hi), src in zip(CHUNKS, banks):
                    last = nc.scalar.activation(fin[:, max(lo - BASE, 0):hi - BASE], src, ACT.Identity,
                                                bias=fin_shift[:, t:t + 1], scale=fin_scale[:, t:t + 1])
                last.then_inc(banks_read, 1)

            act.sem_inc(banks_read, CREDIT)
            for free in (hct_lo_ready, added, stored):
                act.sem_inc(free, 1)
            for dst, src in ((wp_raw, wp_t), (wg_raw, wg_t)):
                act.dma_start(dst, src.rearrange("(t p) c -> p t c", p=P)).then_inc(wp_wg_loaded, 16)
            act.dma_start(gates[:, :], g_both.partition_broadcast(P)).then_inc(small_loaded, 16)
            act.dma_start(wt_raw, wt.rearrange("(t p) c -> p t c", p=P)).then_inc(wt_wz_loaded, 16)
            act.wait_ge(wz_cleared, 1)
            for q in range(P // CG):
                act.dma_start(wz_raw[q * CG:(q + 1) * CG, :, q * CG:(q + 1) * CG],
                              wz_t.rearrange("(t q) i o -> q i t o", t=T)[q]).then_inc(wt_wz_loaded, 16)

            def stage_high(n):
                act.wait_ge(stage_loaded[n % NSTAGE], 16 * (n // NSTAGE + 1))
                hi = stage_parts(n)[0]
                nc.scalar.activation(hi, stage[n % NSTAGE][:, 0:hi.shape[1]], ACT.Copy).then_inc(w_hi_ready, 1)

            act.wait_ge(small_loaded, 16)
            nc.scalar.activation(tg[:, :], gates[:, :], ACT.Tanh).then_inc(tanh_done, 1)
            act.wait_ge(wp_wg_loaded, 32)
            nc.scalar.activation(w_p[0][:, :, :], wp_raw, ACT.Copy).then_inc(wp_wg_hi, 1)
            nc.scalar.activation(w_g[0][:, :, :], wg_raw, ACT.Copy).then_inc(wp_wg_hi, 1)
            x_high(0, 0, xn[:, :])
            x_high(0, 1, y0[:, 1, :])
            ctx_high(0, 0)
            ctx_high(0, 1)
            act.wait_ge(m_done, 1)
            nc.scalar.activation(w_m[0][:, :, :], bank[0][:, :].rearrange("p (t c) -> p t c", t=T), ACT.Copy)\
                .then_inc(wm_hi, 1)
            for n in range(PAIRS):
                stage_high(n)
                g_copy(0, n)
            for n in range(PAIRS):
                stage_high(PAIRS + n)
                y_copy(0, n)
                if n == 1:
                    x_high(1, 0, xn[:, :])
            ctx_high(1, 0)
            ctx_high(1, 1)
            x_high(1, 1, xn[:, :])
            stage_high(SPLITS - 1)
            x1_center(0)

            def step(i, prepare):
                for n in range(PAIRS):
                    g_copy(i, n)
                    if n in (1, 2):
                        xt_high(i - 1, 2 * n - 2)
                        xt_high(i - 1, 2 * n - 1)
                for n in range(PAIRS):
                    y_copy(i, n)
                    if n == 1 and prepare:
                        x_high(i + 1, 0, xn[:, :])
                if prepare:
                    ctx_high(i + 1, 0)
                    ctx_high(i + 1, 1)
                    x_high(i + 1, 1, xn[:, :])
                exps(i - 1, 0)
                exps(i - 1, 1)
                hct_high(i - 1, 0)
                finish(i - 1, 0)
                x1_center(i)
                hct_high(i - 1, 1)
                finish(i - 1, 1)

            with act.Fori(1, NB - 1) as i:
                step(i, True)
            step(NB - 1, False)
            for q in range(NQ):
                xt_high(NB - 1, q)
            exps(NB - 1, 0)
            exps(NB - 1, 1)
            hct_high(NB - 1, 0)
            finish(NB - 1, 0)
            hct_high(NB - 1, 1)
            finish(NB - 1, 1)

        @block.vector
        def _(dve):
            def x_stat(b, t):
                dve.wait_ge(x_loaded[t], count(16, b, 16))
                for h in range(HALVES):
                    last = nc.vector.bn_stats(x_stats[:, t, h, :], x_raw[:, t, h * NF:(h + 1) * NF])
                if t == T - 1:
                    last.then_inc(x_chain, 1)

            def x_scalars(b):
                dve.wait_ge(x_chain, count(2, b, 1))
                nc.vector.memset(carrier[:, :], 0.0)
                for t in range(T):
                    last = nc.vector.bn_aggr(x_mv[:, t, :], x_stats[:, t, :, :])
                last.then_inc(x_chain, 1)
                dve.wait_ge(x_chain, count(2, b, 2))
                nc.vector.tensor_scalar(x_var[:, :], x_mv[:, :, 1], EPS, None, ALU.add).then_inc(x_var_ready, 1)

            def x_norm(b, t, normed):
                if t == 0:
                    dve.wait_ge(x_rstd_ready, count(1, b, 1))
                    dve.wait_ge(att_part, count(PAIRS, b, 0))
                nc.vector.tensor_scalar(normed, x_raw[:, t, :], x_mv[:, t, 0:1], x_rstd[:, t:t + 1],
                                        ALU.subtract, ALU.mult).then_inc(xn_ready, 1)

            def x_low(b, t, normed):
                dve.wait_ge(x_hi_ready, count(T, b, t + 1))
                nc.vector.tensor_tensor(xs[1][:, t, :], normed, xs[0][:, t, :].bitcast(F32), ALU.subtract)\
                    .then_inc(x_lo_ready, 1)

            def sum_inputs(b):
                dve.wait_ge(ctx_loaded, count(16, b, 16))
                for t in range(T):
                    nc.vector.scalar_tensor_tensor(w_sum[:, t, :], ctx_raw[:, t, :], tg[:, 0:1], x_raw[:, t, :],
                                                   ALU.mult, ALU.add).then_inc(w_sum_ready, 1)

            def att_sum(b, n):
                m, h = n // HALVES, n % HALVES
                dve.wait_ge(p_done, count(PAIRS, b, n + 1))
                dve.wait_ge(g_copied, count(PAIRS, b, n + 1))
                g = g_sb[:, n % 2, :]
                nc.vector.tensor_tensor_reduce(g, p_bank[n % 2][:, :], g, 1.0, 0.0, ALU.mult, ALU.add,
                                               row_sums[:, m, h:h + 1]).then_inc(att_part, 1)

            def y_stat(b):
                for n in range(PAIRS):
                    m, h = n // HALVES, n % HALVES
                    dve.wait_ge(y_copied, count(PAIRS, b, n + 1))
                    last = nc.vector.bn_stats(y_stats[:, m, h, :], y0[:, m, h * NF:(h + 1) * NF])
                last.then_inc(y_chain, 1)
                dve.wait_ge(y_chain, count(1, b, 1))
                nc.vector.memset(carrier[:, :], 0.0)
                for m in range(T):
                    last = nc.vector.bn_aggr(row_sums[:, m, 2:4], y_stats[:, m, :, :])
                last.then_inc(means_ready, 1)

            def group_means(b):
                def link(ins, k):
                    ins.then_inc(gn_chain, 1)
                    dve.wait_ge(gn_chain, count(6, b, k))
                sums = bank[0][:, 0:3 * T].rearrange("p (t k) -> p t k", t=T)
                dve.wait_ge(means_summed, count(1, b, 1))
                nc.vector.tensor_reduce(att[:, :], sums[:, :, 0:2], AX.X, ALU.add)
                link(nc.vector.tensor_scalar(g_mean[:, :], sums[:, :, 2], 1.0 / CG, None, ALU.mult), 1)
                nc.vector.tensor_tensor(att2[:, :], att[:, :], att[:, :], ALU.mult)
                link(nc.vector.tensor_tensor(dev[:, :], row_sums[:, :, 2], g_mean[:, :], ALU.subtract), 2)
                nc.vector.tensor_tensor(att_w[:, :], att[:, :], gn_tg[:, 0, :], ALU.mult)
                link(nc.vector.tensor_tensor(dev2[:, :], dev[:, :], dev[:, :], ALU.mult), 3)
                nc.vector.tensor_tensor(row_var[:, :], dev2[:, :], row_sums[:, :, 3], ALU.add)\
                    .then_inc(vars_ready, 1)

            def group_scalars(b):
                def link(ins, k):
                    ins.then_inc(gn_chain, 1)
                    dve.wait_ge(gn_chain, count(6, b, k))
                dve.wait_ge(vars_summed, count(1, b, 1))
                link(nc.vector.scalar_tensor_tensor(g_var[:, :], bank[0][:, 0:T], 1.0 / CG, att2[:, :],
                                                    ALU.mult, ALU.mult), 4)
                nc.vector.tensor_scalar(g_var_eps[:, :], g_var[:, :], EPS, None, ALU.add)\
                    .then_inc(g_var_ready, 1)
                dve.wait_ge(g_rstd_ready, count(1, b, 1))
                link(nc.vector.tensor_tensor(gn_scale[:, :], att_w[:, :], g_rstd[:, :], ALU.mult), 5)
                link(nc.vector.tensor_tensor(gn_drop[:, :], gn_scale[:, :], g_mean[:, :], ALU.mult), 6)
                nc.vector.tensor_tensor(gn_shift[:, :], gn_tg[:, 1, :], gn_drop[:, :], ALU.subtract)

            def x1_sum(b):
                dve.wait_ge(w_sum_ready, count(T, b, T))
                dve.wait_ge(x1c_ready, count(T, b, 0))
                dve.wait_ge(resid_ready, count(T, b, 0))
                for t in range(T):
                    nc.vector.scalar_tensor_tensor(x1[:, t, :], y0[:, t, :], gn_scale[:, t:t + 1],
                                                   w_sum[:, t, :], ALU.mult, ALU.add).then_inc(x1_ready, 1)

            def x1_stat(b):
                for t in range(T):
                    dve.wait_ge(x1_ready, count(T, b, t + 1))
                    for h in range(HALVES):
                        last = nc.vector.bn_stats(x1_stats[:, t, h, :], x1[:, t, h * NF:(h + 1) * NF])
                last.then_inc(x1_chain, 1)
                dve.wait_ge(x1_chain, count(2, b, 1))
                nc.vector.memset(carrier[:, :], 0.0)
                for t in range(T):
                    last = nc.vector.bn_aggr(x1_mv[:, t, :], x1_stats[:, t, :, :])
                last.then_inc(x1_chain, 1)
                dve.wait_ge(x1_chain, count(2, b, 2))
                nc.vector.tensor_scalar(x1_neg_mean[:, :], x1_mv[:, :, 0], -1.0, None, ALU.mult)
                nc.vector.tensor_scalar(x1_var[:, :], x1_mv[:, :, 1], EPS, None, ALU.add)\
                    .then_inc(x1_var_ready, 1)

            def xt_low(b, q):
                t, h = q // 2, q % 2
                at = (slice(None), slice(h * QB, (h + 1) * QB), slice(t * P, (t + 1) * P))
                dve.wait_ge(xt_hi_ready, count(NQ, b, q + 1))
                nc.vector.tensor_tensor(xt[1][at], tr_bank[q % 2][:, :].rearrange("p (k n) -> p k n", k=QB),
                                        xt[0][at].bitcast(F32), ALU.subtract).then_inc(xt_lo_ready, 1)

            def fin_scalars(b):
                dve.wait_ge(x1_rstd_ready, count(1, b, 1))
                dve.wait_ge(banks_read, banks_read_by(b - 1, T - 1))
                nc.vector.tensor_scalar(fin_scale[:, :], x1_rstd[:, :], tg[:, 1:2], None, ALU.mult)
                nc.vector.tensor_copy(fin_shift[:, :], gn_shift[:, :]).then_inc(fin_scalars_ready, 1)

            def gate(b, t):
                def link(ins, k):
                    ins.then_inc(gate_chain, 1)
                    dve.wait_ge(gate_chain, count(7 * T, b, 7 * t + k))
                dve.wait_ge(first_done, count(T, b, t + 1))
                link(nc.vector.tensor_scalar(logit[:, t, :], first_bank[t][:, ER:BASE], x1_rstd[:, t:t + 1],
                                             None, ALU.mult), 1)
                nc.vector.tensor_reduce(neg_max[:, t:t + 1], logit[:, t, :], AX.X, ALU.max, negate=True)\
                    .then_inc(gate_in_ready, 1)
                link(nc.vector.tensor_tensor(diff[:, t, :, :],
                                             logit[:, t, :].unsqueeze(1).broadcast_to((P, E, E)),
                                             logit[:, t, :].unsqueeze(2).broadcast_to((P, E, E)),
                                             ALU.subtract), 2)
                link(nc.vector.tensor_tensor(beats[:, t, :, :], diff[:, t, :, :], tie[:, :, :], ALU.is_ge), 3)
                link(nc.vector.tensor_reduce(rank[:, t, :], beats[:, t, :, :], AX.X, ALU.add), 4)
                dve.wait_ge(exp_done, count(T, b, t + 1))
                link(nc.vector.scalar_tensor_tensor(top[:, t, :], rank[:, t, :], TOP_K - 0.5, prob[:, t, :],
                                                    ALU.is_lt, ALU.mult, accum_out=top_sum[:, t:t + 1]), 5)
                link(nc.vector.reciprocal(top_inv[:, t:t + 1], top_sum[:, t:t + 1]), 6)
                link(nc.vector.tensor_scalar(combine[:, t, :], top[:, t, :], top_inv[:, t:t + 1], LORA_SCALE,
                                             ALU.mult, ALU.mult), 7)
                nc.vector.tensor_tensor(hc[:, t, :].rearrange("p (e r) -> p e r", e=E),
                                        first_bank[t][:, 0:ER].rearrange("p (e r) -> p e r", e=E),
                                        combine[:, t, :].unsqueeze(2).broadcast_to((P, E, R)),
                                        ALU.mult).then_inc(hc_ready, 1)

            def hct_low(b, t):
                dve.wait_ge(hct_hi_ready, count(T, b, t + 1))
                nc.vector.tensor_tensor(hct[1][:, t, :], tr_bank[1][:, 0:P], hct[0][:, t, :].bitcast(F32),
                                        ALU.subtract).then_inc(hct_lo_ready, 1)

            nc.vector.memset(wz_raw, 0.0).then_inc(wz_cleared, 1)
            nc.vector.memset(group_ones[:, :], 0.0)
            nc.vector.memset(tie[:, :, :], TINY).then_inc(consts_filled, 1)
            nc.vector.memset(minus_half[:, :], -0.5).then_inc(consts_ready, 1)
            x_stat(0, 0)
            x_stat(0, 1)
            x_scalars(0)
            dve.wait_ge(consts_filled, 1)
            for q in range(P // CG):
                nc.vector.memset(group_ones[q * CG:(q + 1) * CG, q * CG:(q + 1) * CG], 1.0)
            for e in range(1, E):
                nc.vector.memset(tie[:, e, 0:e], 0.0)
            def ctx_low(b, t):
                dve.wait_ge(c_hi_ready, count(T, b, t + 1))
                nc.vector.tensor_tensor(cs[1][:, t, :], ctx_raw[:, t, :], cs[0][:, t, :].bitcast(F32),
                                        ALU.subtract).then_inc(c_lo_ready, 1)

            def stage_low(n):
                dve.wait_ge(w_hi_ready, n + 1)
                hi, lo = stage_parts(n)
                nc.vector.tensor_tensor(lo, stage[n % NSTAGE][:, 0:lo.shape[1]], hi.bitcast(F32), ALU.subtract)\
                    .then_inc(stage_split[n % NSTAGE], 1)

            dve.wait_ge(wp_wg_hi, 2)
            for parts, whole in ((w_p, wp_raw), (w_g, wg_raw)):
                last = nc.vector.tensor_tensor(parts[1][:, :, :], whole, parts[0][:, :, :].bitcast(F32),
                                               ALU.subtract)
            last.then_inc(wp_wg_ready, 1)
            x_norm(0, 0, xn[:, :])
            x_norm(0, 1, y0[:, 1, :])
            x_low(0, 0, xn[:, :])
            x_low(0, 1, y0[:, 1, :])
            ctx_low(0, 0)
            dve.wait_ge(wm_hi, 1)
            nc.vector.tensor_tensor(w_m[1][:, :, :], bank[0][:, :].rearrange("p (t c) -> p t c", t=T),
                                    w_m[0][:, :, :].bitcast(F32), ALU.subtract).then_inc(wm_ready, 1)
            dve.wait_ge(tanh_done, 1)
            sum_inputs(0)
            dve.wait_ge(gn_loaded, 16)
            nc.vector.tensor_scalar(gn_tg[:, :, :], gn_wb[:, :, :], tg[:, 0:1], None, ALU.mult)\
                .then_inc(gn_tg_ready, 1)
            att_sum(0, 0)
            stage_low(2)
            att_sum(0, 1)
            x_stat(1, 0)
            att_sum(0, 2)
            x_stat(1, 1)
            x_scalars(1)
            att_sum(0, 3)
            x_norm(1, 0, xn[:, :])
            stage_low(5)
            dve.wait_ge(bias_loaded, 16)
            nc.vector.tensor_scalar(tf_bias[:, :], tf_bias[:, :], tg[:, 1:2], None, ALU.mult)\
                .then_inc(tf_bias_ready, 1)
            y_stat(0)
            x_low(1, 0, xn[:, :])
            dve.wait_ge(x_lo_ready, count(T, 1, 1))
            x_norm(1, 1, xn[:, :])
            dve.wait_ge(gn_tg_ready, 1)
            group_means(0)
            ctx_low(1, 0)
            x_low(1, 1, xn[:, :])
            group_scalars(0)
            stage_low(8)
            dve.wait_ge(stage_split[2], SPLITS // NSTAGE)
            x1_sum(0)
            x1_stat(0)
            sum_inputs(1)

            def step(i, prepare):
                for n in range(PAIRS):
                    att_sum(i, n)
                    if n in (1, 2):
                        xt_low(i - 1, 2 * n - 2)
                        xt_low(i - 1, 2 * n - 1)
                        if prepare:
                            x_stat(i + 1, n - 1)
                if prepare:
                    x_scalars(i + 1)
                if prepare:
                    x_norm(i + 1, 0, xn[:, :])
                y_stat(i)
                if prepare:
                    x_low(i + 1, 0, xn[:, :])
                    dve.wait_ge(x_lo_ready, count(T, i + 1, 1))
                    x_norm(i + 1, 1, xn[:, :])
                fin_scalars(i - 1)
                gate(i - 1, 0)
                if prepare:
                    x_low(i + 1, 1, xn[:, :])
                gate(i - 1, 1)
                group_means(i)
                hct_low(i - 1, 0)
                group_scalars(i)
                x1_sum(i)
                x1_stat(i)
                hct_low(i - 1, 1)
                if prepare:
                    sum_inputs(i + 1)

            with dve.Fori(1, NB - 1) as i:
                step(i, True)
            step(NB - 1, False)
            for q in range(NQ):
                xt_low(NB - 1, q)
            fin_scalars(NB - 1)
            gate(NB - 1, 0)
            gate(NB - 1, 1)
            hct_low(NB - 1, 0)
            hct_low(NB - 1, 1)

        @block.tensor
        def _(pe):
            def product(dst, weights, w_at, moving, m_at, steps):
                for k in range(steps):
                    for a, c in PARTS:
                        last = nc.tensor.matmul(dst, w_at(weights[a], k), m_at(moving[c], k),
                                                start=(k == 0 and (a, c) == PARTS[0]),
                                                stop=(k == steps - 1 and (a, c) == PARTS[-1]))
                return last

            def chunk(weights, moving, dst, n):
                m, h = n // HALVES, n % HALVES
                return product(dst, weights, lambda w, k: w[:, k, m * P:(m + 1) * P],
                               moving, lambda v, k: v[:, k, h * NF:(h + 1) * NF], T)

            def pair(b, n):
                if n == 0:
                    pe.wait_ge(x_lo_ready, count(T, b, T))
                if n < 2:
                    pe.wait_ge(banks_read, banks_read_by(b - 2, n))
                else:
                    pe.wait_ge(att_part, count(PAIRS, b, n - 1))
                chunk(w_p, xs, p_bank[n % 2][:, :], n).then_inc(p_done, 1)
                if n == 0:
                    pe.wait_ge(c_lo_ready, count(T, b, T))
                chunk(w_g, cs, g_bank[n % 2][:, :], n).then_inc(g_done, 1)

            def transposes(b, groups):
                for q in groups:
                    t, h = q // 2, q % 2
                    if h == 0:
                        pe.wait_ge(x1c_ready, count(T, b, t + 1))
                    if q == 0:
                        pe.wait_ge(g_var_ready, count(1, b, 1))
                    elif q == 1:
                        pe.wait_ge(hct_lo_ready, credited(T, b, 0))
                    else:
                        pe.wait_ge(xt_lo_ready, count(NQ, b, q - 1))
                    for j in range(QB):
                        k = h * QB + j
                        last = nc.tensor.transpose(tr_bank[q % 2][:, j * P:(j + 1) * P],
                                                   y0[:, t, k * P:(k + 1) * P], ident[:, :])
                    last.then_inc(xt_done, 1)

            def y_products(b):
                for n in range(PAIRS):
                    pe.wait_ge(att_part, count(PAIRS, b, 3 + n // 2))
                    chunk(w_m, cs, y_bank[n][:, :], n).then_inc(y_done, 1)

            def ffn_chunk(b, t, dst, n):
                lo, hi = CHUNKS[n]
                return product(dst, xt, lambda w, k: w[:, k, t * P:(t + 1) * P],
                               w_ext, lambda v, k: v[:, k, lo:hi], KD)

            def first_chunk(b, t):
                pe.wait_ge(xt_lo_ready, count(NQ, b, 2 * t + 2))
                pe.wait_ge(banks_read, banks_read_by(b - 1, t))
                if t == 0:
                    for split_done in stage_split:
                        pe.wait_ge(split_done, SPLITS // NSTAGE)
                ffn_chunk(b, t, first_bank[t][:, 0:CHUNKS[0][1]], 0).then_inc(first_done, 1)

            def sum_means(b, ffn):
                pe.wait_ge(means_ready, count(1, b, 1))
                if ffn:
                    pe.wait_ge(xt_lo_ready, count(NQ, b - 1, 3))
                nc.tensor.matmul(bank[0][:, 0:3 * T].rearrange("p (t k) -> p t k", t=T), group_ones[:, :],
                                 row_sums[:, :, 0:3], start=True, stop=True).then_inc(means_summed, 1)

            def sum_vars(b):
                pe.wait_ge(vars_ready, count(1, b, 1))
                nc.tensor.matmul(bank[0][:, 0:T], group_ones[:, :], row_var[:, :], start=True, stop=True)\
                    .then_inc(vars_summed, 1)

            def rest(b, t, beside, ffn_attention):
                width = [hi - lo for lo, hi in CHUNKS]
                for n in range(2):
                    if ffn_attention:
                        pe.wait_ge(y_copied, count(PAIRS, b + 1, 2 * t + n + 1))
                    ffn_chunk(b, t, rest_bank[t][n][:, 0:width[n + 1]], n + 1)
                    if n == 0:
                        pe.wait_ge(hc_ready, count(T, b, t + 1))
                        if t == 0:
                            pe.wait_ge(xt_lo_ready, count(NQ, b, NQ))
                        else:
                            pe.wait_ge(hct_lo_ready, credited(T, b, t))
                        nc.tensor.transpose(tr_bank[1][:, 0:P], hc[:, t, :], ident[:, :]).then_inc(hct_done, 1)
                        beside()
                pe.wait_ge(hct_lo_ready, credited(T, b, t + 1))
                dsts = [first_bank[t][:, BASE:width[0]], rest_bank[t][0][:, 0:width[1]],
                        rest_bank[t][1][:, 0:width[2]]]
                for (lo, hi), dst in zip(CHUNKS, dsts):
                    for a, c in PARTS:
                        last = nc.tensor.matmul(dst, hct[a][:, t, :], b_up[c][:, max(lo - BASE, 0):hi - BASE],
                                                start=False, stop=True, skip_group_check=True)
                last.then_inc(ffn_done, 1)

            pe.wait_ge(wt_wz_loaded, 16 * (1 + P // CG))
            for m in range(T):
                for k in range(T):
                    last = nc.tensor.matmul(bank[0][:, m * C + k * P:m * C + (k + 1) * P],
                                            wt_raw[:, k, m * P:(m + 1) * P], wz_raw[:, k, :],
                                            start=True, stop=True)
            last.then_inc(m_done, 1)
            pe.wait_ge(wp_wg_ready, 1)
            for n in range(PAIRS):
                pair(0, n)
            pe.wait_ge(wm_ready, 1)
            y_products(0)
            sum_means(0, False)
            sum_vars(0)
            pe.wait_ge(ident_ready, 1)

            with pe.Fori(1, NB) as i:
                pair(i, 0)
                pair(i, 1)
                transposes(i - 1, (0, 1))
                pair(i, 2)
                transposes(i - 1, (2, 3))
                pair(i, 3)
                y_products(i)
                first_chunk(i - 1, 0)
                first_chunk(i - 1, 1)
                sum_means(i, True)
                rest(i - 1, 0, lambda: sum_vars(i), True)
                rest(i - 1, 1, lambda: None, True)
            transposes(NB - 1, range(NQ))
            first_chunk(NB - 1, 0)
            first_chunk(NB - 1, 1)
            rest(NB - 1, 0, lambda: None, False)
            rest(NB - 1, 1, lambda: None, False)


_OUT_SHAPE = (8, 256, 1024)


def kernel(x, ctx_4096, g_xattn, g_ffn, L0_xattn_Wt, L0_xattn_Wp, L0_xattn_Wg, L0_xattn_Wz, L0_xattn_gn_w,
           L0_xattn_gn_b, L0_ffn_W_base, L0_ffn_b_base, L0_ffn_W_router, L0_ffn_A_stack, L0_ffn_B_stack):
    import numpy as np
    import concourse.bacc as bacc
    from concourse.bass_utils import run_bass_kernel_spmd

    groups = 8
    cg = L0_xattn_Wz.shape[1]
    experts, rank, d = L0_ffn_A_stack.shape
    a_rows = np.asarray(L0_ffn_A_stack).reshape(experts * rank, d)
    w_rows = np.concatenate([a_rows, np.asarray(L0_ffn_W_router), np.asarray(L0_ffn_W_base)], axis=0)
    arrays = {
        "x": x, "ctx": ctx_4096, "g_both": np.concatenate([g_xattn, g_ffn]),
        "wt": L0_xattn_Wt, "wp_t": np.asarray(L0_xattn_Wp).T, "wg_t": np.asarray(L0_xattn_Wg).T,
        "wz_t": np.asarray(L0_xattn_Wz).reshape(groups, cg, cg).transpose(0, 2, 1),
        "gn_cols": np.stack([L0_xattn_gn_w, L0_xattn_gn_b]).reshape(2, -1, P).transpose(2, 0, 1),
        "w_ext_t": w_rows.T, "b_base": L0_ffn_b_base,
        "b_stack_t": np.asarray(L0_ffn_B_stack).transpose(0, 2, 1).reshape(experts * rank, -1),
    }
    nc = bacc.Bacc("TRN2", target_bir_lowering=False, num_devices=1)
    feeds, args = {}, []
    for name, a in arrays.items():
        a = np.ascontiguousarray(a)
        feeds[f"in_{name}"] = a
        args.append(nc.dram_tensor(f"in_{name}", a.shape, mybir.dt.from_np(a.dtype), kind="ExternalInput").ap())
    out = nc.dram_tensor("out", _OUT_SHAPE, F32, kind="ExternalOutput").ap()
    gated_block_kernel(nc, *args, out)
    r = run_bass_kernel_spmd(nc, [feeds], core_ids=[0])
    return r.results[0]["out"]
```

```python
from contextlib import ExitStack

import concourse.bass as bass
from concourse import mybir

ALU = mybir.AluOpType
ACT = mybir.ActivationFunctionType
AX = mybir.AxisListType
F32 = mybir.dt.float32
F32R = mybir.dt.float32r

P = 128
EPS = 1e-5
TOP_K = 2
TINY = 1.2e-38


def gated_block_kernel(nc, x, ctx, g_both, wt, wp_t, wg_t, wz_t, gn_cols,
                       w_ext_t, b_base, b_stack_t, out):
    NB, C, D = x.shape
    T = C // P
    GROUPS, CG = wz_t.shape[0], wz_t.shape[1]
    NF = 512
    HALVES = D // NF
    PAIRS = T * HALVES
    KD = D // P
    WEXT = w_ext_t.shape[1]
    ER = b_stack_t.shape[0]
    E = WEXT - ER - D
    R = ER // E
    LORA_SCALE = 32.0 / R
    BASE = ER + E
    CHUNKS = [(0, BASE + 256), (BASE + 256, BASE + 640), (BASE + 640, WEXT)]
    NQ = 2 * T
    QB = KD // 2
    KH = KD // 2
    PIECES = 2 * len(CHUNKS) + 1
    PARTS = ((0, 0), (1, 0), (0, 1))
    assert T == 2 and HALVES == 2 and CG == 32 and ER == P and KD == 8

    x_v = x.rearrange("b (t p) d -> b p t d", p=P)
    ctx_v = ctx.rearrange("b (t p) d -> b p t d", p=P)
    out_v = out.rearrange("b (t p) d -> b p t d", p=P)

    with ExitStack() as stack:
        def sb(name, shape, dt=F32):
            return stack.enter_context(nc.sbuf_tensor(name, shape, dt))

        def sem(name):
            return stack.enter_context(nc.semaphore(name))

        def split(name, shape):
            return [sb(name + "_hi", shape, F32R), sb(name + "_lo", shape, F32R)]

        w_ext = split("w_ext", [P, KD, WEXT])
        b_up = split("b_up", [P, D])
        w_m = split("w_m", [P, T, C])
        w_p = split("w_p", [P, T, C])
        w_g = split("w_g", [P, T, C])
        tf_bias = sb("tf_bias", [P, D])
        x_raw = sb("x_raw", [P, T, D])
        ctx_raw = sb("ctx_raw", [P, T, D])
        xn = sb("xn", [P, D])
        g_sb = xn[:, :].rearrange("p (s n) -> p s n", s=2)
        xs = split("xs", [P, T, D])
        cs = split("cs", [P, T, D])
        w_sum = sb("w_sum", [P, T, D])
        y0 = sb("y0", [P, T, D])
        x1 = sb("x1", [P, T, D])
        xt = split("xt", [P, KD, C])
        late = sb("late", [P, max(T * D + D, 2 * KH * (BASE + 256))])
        resid = late[:, 0:T * D].rearrange("p (t d) -> p t d", t=T)
        fin = late[:, T * D:T * D + D]
        hc = sb("hc", [P, T, ER])
        hct = split("hct", [P, T, P])
        raw = x1[:, :, :].rearrange("p t d -> p (t d)")
        wt_raw = raw[:, 0:T * C].rearrange("p (t c) -> p t c", t=T)
        wz_raw = raw[:, T * C:T * C + T * CG].rearrange("p (t c) -> p t c", t=T)
        early_xn = [x1[:, t, :] for t in range(T)]
        WPLACE = KH * max(hi - lo for lo, hi in CHUNKS)
        place = [late[:, n * WPLACE:(n + 1) * WPLACE] for n in range(2)]
        wg_raw, wp_raw = [at[:, 0:T * C].rearrange("p (t c) -> p t c", t=T) for at in place]
        wz_diag = y0[:, 0, 0:T * P].rearrange("p (t c) -> p t c", t=T)
        ident = sb("ident", [P, P])
        group_ones = sb("group_ones", [P, P])
        tie = sb("tie", [P, E, E])
        minus_half = sb("minus_half", [P, T])
        gates = sb("gates", [P, 2])
        tg = sb("tg", [P, 2])
        gn_wb = sb("gn_wb", [P, 2, T])
        gn_tg = sb("gn_tg", [P, 2, T])
        carrier = sb("carrier", [P, 2 * T + 1])
        x_stats = sb("x_stats", [P, T, HALVES, 6])
        x_mv = sb("x_mv", [P, T, 2])
        x_var = sb("x_var", [P, T])
        x_rstd = sb("x_rstd", [P, T])
        y_stats = sb("y_stats", [P, T, HALVES, 6])
        row_sums = sb("row_sums", [P, T, 4])
        att = sb("att", [P, T])
        g_mean = sb("g_mean", [P, T])
        dev = sb("dev", [P, T])
        dev2 = sb("dev2", [P, T])
        row_var = sb("row_var", [P, T])
        att2 = sb("att2", [P, T])
        att_w = sb("att_w", [P, T])
        g_var = sb("g_var", [P, T])
        g_var_eps = sb("g_var_eps", [P, T])
        g_rstd = sb("g_rstd", [P, T])
        gn_scale = sb("gn_scale", [P, T])
        gn_drop = sb("gn_drop", [P, T])
        gn_shift = sb("gn_shift", [P, T])
        x1_stats = sb("x1_stats", [P, T, HALVES, 6])
        x1_mv = sb("x1_mv", [P, T, 2])
        x1_neg_mean = sb("x1_neg_mean", [P, T])
        x1_var = sb("x1_var", [P, T])
        x1_rstd = sb("x1_rstd", [P, T])
        fin_scale = sb("fin_scale", [P, T])
        fin_shift = sb("fin_shift", [P, T])
        logit = sb("logit", [P, T, E])
        neg_max = sb("neg_max", [P, T])
        prob = sb("prob", [P, T, E])
        diff = sb("diff", [P, T, E, E])
        beats = sb("beats", [P, T, E, E])
        rank = sb("rank", [P, T, E])
        top = sb("top", [P, T, E])
        top_sum = sb("top_sum", [P, T])
        top_inv = sb("top_inv", [P, T])
        combine = sb("combine", [P, T, E])

        bank = [stack.enter_context(nc.psum_tensor(f"bank{n}", [P, NF], F32)) for n in range(8)]
        tr_bank = [bank[0], bank[1]]
        first_bank = [bank[2], bank[3]]
        p_bank, g_bank = [bank[4], bank[6]], [bank[5], bank[7]]
        y_bank = [bank[4], bank[5], bank[6], bank[7]]
        rest_bank = [[bank[4], bank[5]], [bank[6], bank[7]]]

        small_loaded = sem("small_loaded")
        gn_loaded = sem("gn_loaded")
        wz_cleared = sem("wz_cleared")
        wz_placed = sem("wz_placed")
        wp_loaded = sem("wp_loaded")
        wg_loaded = sem("wg_loaded")
        wt_wz_loaded = sem("wt_wz_loaded")
        bias_loaded = sem("bias_loaded")
        piece_loaded = [sem(f"place{n}_loaded") for n in range(2)]
        piece_split = [sem(f"place{n}_split") for n in range(2)]
        tanh_done = sem("tanh_done")
        consts_ready = sem("consts_ready")
        consts_filled = sem("consts_filled")
        ident_zeroed = sem("ident_zeroed")
        ident_ready = sem("ident_ready")
        m_done = sem("m_done")
        wp_hi = sem("wp_hi")
        wg_hi = sem("wg_hi")
        wp_ready = sem("wp_ready")
        wg_ready = sem("wg_ready")
        wm_hi = sem("wm_hi")
        wm_ready = sem("wm_ready")
        piece_hi = sem("piece_hi")
        gn_tg_ready = sem("gn_tg_ready")
        tf_bias_ready = sem("tf_bias_ready")
        x_loaded = [sem(f"x{t}_loaded") for t in range(T)]
        ctx_loaded = [sem(f"ctx{t}_loaded") for t in range(T)]
        x_var_ready = sem("x_var_ready")
        x_rstd_ready = sem("x_rstd_ready")
        xn_ready = sem("xn_ready")
        x_hi_ready = sem("x_hi_ready")
        x_lo_ready = sem("x_lo_ready")
        c_hi_ready = sem("c_hi_ready")
        c_lo_ready = sem("c_lo_ready")
        w_sum_ready = sem("w_sum_ready")
        p_done = sem("p_done")
        g_done = sem("g_done")
        g_copied = sem("g_copied")
        att_part = sem("att_part")
        y_done = sem("y_done")
        y_copied = sem("y_copied")
        means_ready = sem("means_ready")
        means_summed = sem("means_summed")
        vars_ready = sem("vars_ready")
        vars_summed = sem("vars_summed")
        g_var_ready = sem("g_var_ready")
        g_rstd_ready = sem("g_rstd_ready")
        x1_ready = sem("x1_ready")
        x1_var_ready = sem("x1_var_ready")
        x1_rstd_ready = sem("x1_rstd_ready")
        x1c_ready = sem("x1c_ready")
        resid_ready = sem("resid_ready")
        xt_done = sem("xt_done")
        xt_hi_ready = sem("xt_hi_ready")
        xt_lo_ready = sem("xt_lo_ready")
        first_done = sem("first_done")
        fin_scalars_ready = sem("fin_scalars_ready")
        gate_in_ready = sem("gate_in_ready")
        exp_done = sem("exp_done")
        hc_ready = sem("hc_ready")
        hct_done = sem("hct_done")
        hct_hi_ready = sem("hct_hi_ready")
        hct_lo_ready = sem("hct_lo_ready")
        ffn_done = sem("ffn_done")
        banks_read = sem("banks_read")
        added = sem("added")
        stored = sem("stored")
        CREDIT = 2 * T
        tail_done = sem("tail_done")
        tail_scaled = sem("tail_scaled")
        tail_added = sem("tail_added")
        x_stats_done = sem("x_stats_done")
        x_mv_done = sem("x_mv_done")
        y_chain = sem("y_chain")
        gn_chain = sem("gn_chain")
        x1_chain = sem("x1_chain")
        gate_chain = sem("gate_chain")

        def opening(b):
            return isinstance(b, int) and b == 0

        def count(per_batch, b, k):
            return per_batch * b + k

        def credited(per_batch, b, k):
            return 1 + count(per_batch, b, k)

        def banks_read_by(b, t):
            return CREDIT + T * b + t + 1

        def piece_parts(n):
            if n == PIECES - 1:
                return [w[:, :] for w in b_up]
            (lo, hi), k = CHUNKS[n // 2], n % 2 * KH
            return [w[:, k:k + KH, lo:hi] for w in w_ext]

        def piece_raw(n):
            if n == PIECES - 1:
                return place[n % 2][:, 0:D]
            lo, hi = CHUNKS[n // 2]
            return place[n % 2][:, 0:KH * (hi - lo)].rearrange("p (k n) -> p k n", k=KH)

        def xt_bank(b, q):
            last = isinstance(b, int) and b == NB - 1
            return (tr_bank + rest_bank[0])[q] if last else tr_bank[q % 2]

        block = stack.enter_context(nc.Block())

        @block.sync
        def _(sp):
            def load_ctx(b, t):
                sp.dma_start(ctx_raw[:, t, :], ctx_v[b][:, t, :]).then_inc(ctx_loaded[t], 16)

            def load_x(b, t):
                sp.dma_start(x_raw[:, t, :], x_v[b][:, t, :]).then_inc(x_loaded[t], 16)

            def load(b):
                sp.wait_ge(w_sum_ready, count(T, b, 0))
                for t in range(T):
                    load_x(b, t)
                sp.wait_ge(c_lo_ready, count(T, b, 0))
                for t in range(T):
                    load_ctx(b, t)

            def store(b, t):
                sp.wait_ge(added, credited(T, b, t + 1))
                sp.dma_start(out_v[b][:, t, :], fin).then_inc(stored, 16)

            def load_piece(n):
                src = b_stack_t
                if n < PIECES - 1:
                    (lo, hi), k = CHUNKS[n // 2], n % 2 * KH
                    src = w_ext_t[k * P:(k + KH) * P, lo:hi].rearrange("(k p) n -> p k n", p=P)
                if n >= 2:
                    sp.wait_ge(piece_split[n % 2], n // 2)
                elif n == 0:
                    sp.wait_ge(wg_ready, 1)
                else:
                    sp.wait_ge(wp_ready, 1)
                sp.dma_start(piece_raw(n), src).then_inc(piece_loaded[n % 2], 16)

            load_ctx(0, 0)
            sp.dma_start(wg_raw, wg_t.rearrange("(t p) c -> p t c", p=P)).then_inc(wg_loaded, 16)
            load_ctx(0, 1)
            load_x(0, 0)
            load_x(0, 1)
            sp.dma_start(wp_raw, wp_t.rearrange("(t p) c -> p t c", p=P)).then_inc(wp_loaded, 16)
            sp.dma_start(gn_wb[:, :, :], gn_cols).then_inc(gn_loaded, 16)
            sp.dma_start(tf_bias[:, :], b_base.partition_broadcast(P)).then_inc(bias_loaded, 16)
            for t in range(T):
                sp.wait_ge(w_sum_ready, t + 1)
                sp.wait_ge(xn_ready, t + 1)
                load_x(1, t)
                sp.wait_ge(c_lo_ready, t + 1)
                load_ctx(1, t)
            for n in range(4):
                load_piece(n)
            sp.wait_ge(w_sum_ready, count(T, 2, 0))
            for t in range(T):
                load_x(2, t)
            for n in range(4, PIECES):
                load_piece(n)
            sp.wait_ge(c_lo_ready, count(T, 2, 0))
            for t in range(T):
                load_ctx(2, t)
            with sp.Fori(1, NB - 2) as i:
                store(i - 1, 0)
                load(i + 2)
                store(i - 1, 1)
            for b in range(NB - 3, NB):
                for t in range(T):
                    if (b, t) != (NB - 1, T - 1):
                        store(b, t)
            for n, (lo, hi) in enumerate(CHUNKS):
                at = slice(max(lo - BASE, 0), hi - BASE)
                sp.wait_ge(tail_added, n + 1)
                sp.dma_start(out_v[NB - 1][:, T - 1, at], fin[:, at]).then_inc(stored, 16)
            sp.wait_ge(stored, credited(16 * T, NB, 16 * (len(CHUNKS) - 1)))

        @block.gpsimd
        def _(pool):
            def rstd_x(b, t):
                at = slice(t, t + 1)
                pool.wait_ge(x_var_ready, count(T, b, t + 1))
                nc.gpsimd.tensor_tensor(x_rstd[:, at], x_var[:, at], minus_half[:, at], ALU.pow)\
                    .then_inc(x_rstd_ready, 1)

            def ctx_low(b, t):
                pool.wait_ge(c_hi_ready, count(T, b, t + 1))
                nc.gpsimd.tensor_tensor(cs[1][:, t, :], ctx_raw[:, t, :], cs[0][:, t, :].bitcast(F32),
                                        ALU.subtract).then_inc(c_lo_ready, 1)

            def rstd_group(b):
                pool.wait_ge(g_var_ready, count(1, b, 1))
                nc.gpsimd.tensor_tensor(g_rstd[:, :], g_var_eps[:, :], minus_half[:, :], ALU.pow)\
                    .then_inc(g_rstd_ready, 1)

            def rstd_x1(b):
                pool.wait_ge(x1_var_ready, count(T, b, T))
                nc.gpsimd.tensor_tensor(x1_rstd[:, :], x1_var[:, :], minus_half[:, :], ALU.pow)\
                    .then_inc(x1_rstd_ready, 1)

            def residual(b):
                pool.wait_ge(added, credited(T, b, 0))
                for t in range(T):
                    pool.wait_ge(x1_ready, count(T, b, t + 1))
                    nc.gpsimd.tensor_tensor(resid[:, t, :], x1[:, t, :], tf_bias[:, :], ALU.add)\
                        .then_inc(resid_ready, 1)

            def add(b, t):
                pool.wait_ge(resid_ready, count(T, b, t + 1))
                pool.wait_ge(banks_read, banks_read_by(b, t))
                nc.gpsimd.tensor_tensor(fin, fin, resid[:, t, :], ALU.add).then_inc(added, 1)

            def x_low(b, t, normed):
                pool.wait_ge(x_hi_ready, count(T, b, t + 1))
                nc.gpsimd.tensor_tensor(xs[1][:, t, :], normed, xs[0][:, t, :].bitcast(F32), ALU.subtract)\
                    .then_inc(x_lo_ready, 1)

            def piece_low(n):
                pool.wait_ge(piece_hi, n + 1)
                hi, lo = piece_parts(n)
                nc.gpsimd.tensor_tensor(lo, piece_raw(n), hi.bitcast(F32), ALU.subtract)\
                    .then_inc(piece_split[n % 2], 1)

            nc.gpsimd.memset(ident[:, :], 0.0).then_inc(ident_zeroed, 1)
            pool.wait_ge(ident_zeroed, 1)
            nc.gpsimd.affine_select(out=ident[:, :], in_=ident[:, :], compare_op=ALU.not_equal, fill=1.0,
                                    base=0, pattern=[[-1, P]], channel_multiplier=1).then_inc(ident_ready, 1)

            pool.wait_ge(consts_ready, 1)
            pool.wait_ge(wg_hi, 1)
            nc.gpsimd.tensor_tensor(w_g[1][:, :, :], wg_raw, w_g[0][:, :, :].bitcast(F32),
                                    ALU.subtract).then_inc(wg_ready, 1)
            rstd_x(0, 0)
            rstd_x(0, 1)
            x_low(0, 0, early_xn[0])
            pool.wait_ge(wp_hi, 1)
            nc.gpsimd.tensor_tensor(w_p[1][:, :, :], wp_raw, w_p[0][:, :, :].bitcast(F32),
                                    ALU.subtract).then_inc(wp_ready, 1)
            rstd_x(1, 0)
            ctx_low(1, 0)
            ctx_low(1, 1)
            rstd_x(1, 1)
            x_low(1, 0, early_xn[0])
            rstd_group(0)
            piece_low(0)
            piece_low(1)
            rstd_x1(0)

            def step(i, prepare):
                residual(i - 1)
                if prepare:
                    for t in range(T):
                        rstd_x(i + 1, t)
                    ctx_low(i + 1, 0)
                    ctx_low(i + 1, 1)
                rstd_group(i)
                add(i - 1, 0)
                rstd_x1(i)
                add(i - 1, 1)

            piece_low(3)
            rstd_x(2, 0)
            rstd_x(2, 1)
            piece_low(5)
            for n in range(2):
                pool.wait_ge(piece_split[n], (PIECES + 1 - n) // 2)
            pool.wait_ge(tf_bias_ready, 1)
            residual(0)
            rstd_group(1)
            add(0, 0)
            ctx_low(2, 0)
            ctx_low(2, 1)
            rstd_x1(1)
            add(0, 1)
            with pool.Fori(2, NB - 1) as i:
                step(i, True)
            step(NB - 1, False)
            residual(NB - 1)
            add(NB - 1, 0)

        @block.scalar
        def _(act):
            def ctx_high(b, t):
                act.wait_ge(ctx_loaded[t], count(16, b, 16))
                if not opening(b):
                    act.wait_ge(y_done, count(PAIRS, b, 0))
                nc.scalar.activation(cs[0][:, t, :], ctx_raw[:, t, :], ACT.Copy).then_inc(c_hi_ready, 1)

            def x_high(b, t, normed):
                act.wait_ge(xn_ready, count(T, b, t + 1))
                if not opening(b):
                    act.wait_ge(p_done, count(PAIRS, b, 0))
                nc.scalar.activation(xs[0][:, t, :], normed, ACT.Copy).then_inc(x_hi_ready, 1)

            def g_copy(b, n):
                act.wait_ge(g_done, count(PAIRS, b, n + 1))
                if n >= 2 or not opening(b):
                    act.wait_ge(att_part, count(PAIRS, b, n - 1))
                nc.scalar.activation(g_sb[:, n % 2, :], g_bank[n % 2][:, :], ACT.Copy).then_inc(g_copied, 1)

            def y_copy(b, n):
                act.wait_ge(y_done, count(PAIRS, b, n + 1))
                m, h = n // HALVES, n % HALVES
                nc.scalar.activation(y0[:, m, h * NF:(h + 1) * NF], y_bank[n][:, :], ACT.Copy)\
                    .then_inc(y_copied, 1)

            def x1_center(b, t):
                act.wait_ge(x1_var_ready, count(T, b, t + 1))
                nc.scalar.activation(y0[:, t, :], x1[:, t, :], ACT.Identity, bias=x1_neg_mean[:, t:t + 1])\
                    .then_inc(x1c_ready, 1)

            def xt_high(b, q):
                t, h = q // 2, q % 2
                act.wait_ge(xt_done, count(NQ, b, q + 1))
                nc.scalar.activation(xt[0][:, h * QB:(h + 1) * QB, t * P:(t + 1) * P],
                                     xt_bank(b, q)[:, :].rearrange("p (k n) -> p k n", k=QB), ACT.Copy)\
                    .then_inc(xt_hi_ready, 1)

            def exps(b, t):
                act.wait_ge(gate_in_ready, count(T, b, t + 1))
                nc.scalar.activation(prob[:, t, :], logit[:, t, :], ACT.Exp, bias=neg_max[:, t:t + 1])\
                    .then_inc(exp_done, 1)

            def hct_high(b, t):
                act.wait_ge(hct_done, count(T, b, t + 1))
                nc.scalar.activation(hct[0][:, t, :], tr_bank[1][:, 0:P], ACT.Copy).then_inc(hct_hi_ready, 1)

            def finish(b, t):
                act.wait_ge(fin_scalars_ready, count(1, b, 1))
                act.wait_ge(stored, credited(16 * T, b, 16 * t))
                act.wait_ge(ffn_done, count(T, b, t + 1))
                banks = [first_bank[t][:, BASE:CHUNKS[0][1]]]
                banks += [rest_bank[t][n][:, 0:CHUNKS[n + 1][1] - CHUNKS[n + 1][0]] for n in range(2)]
                for (lo, hi), src in zip(CHUNKS, banks):
                    last = nc.scalar.activation(fin[:, max(lo - BASE, 0):hi - BASE], src, ACT.Identity,
                                                bias=fin_shift[:, t:t + 1], scale=fin_scale[:, t:t + 1])
                last.then_inc(banks_read, 1)

            def finish_last():
                t = T - 1
                act.wait_ge(stored, credited(16 * T, NB - 1, 16 * t))
                for n, (lo, hi) in enumerate(CHUNKS):
                    src = first_bank[t][:, BASE:hi] if n == 0 else rest_bank[t][n - 1][:, 0:hi - lo]
                    if n < len(CHUNKS) - 1:
                        act.wait_ge(tail_done, n + 1)
                    else:
                        act.wait_ge(ffn_done, T * NB)
                    nc.scalar.activation(fin[:, max(lo - BASE, 0):hi - BASE], src, ACT.Identity,
                                         bias=fin_shift[:, t:t + 1], scale=fin_scale[:, t:t + 1])\
                        .then_inc(tail_scaled, 1)

            def piece_high(n):
                act.wait_ge(piece_loaded[n % 2], 16 * (n // 2 + 1))
                nc.scalar.activation(piece_parts(n)[0], piece_raw(n), ACT.Copy).then_inc(piece_hi, 1)

            act.sem_inc(banks_read, CREDIT)
            for free in (hct_lo_ready, added, stored):
                act.sem_inc(free, 1)
            act.dma_start(wt_raw, wt.rearrange("(t p) c -> p t c", p=P)).then_inc(wt_wz_loaded, 16)
            act.dma_start(wz_raw, wz_t.rearrange("(t q) i o -> (q i) t o", t=T)).then_inc(wt_wz_loaded, 16)
            act.dma_start(gates[:, :], g_both.partition_broadcast(P)).then_inc(small_loaded, 16)

            ctx_high(0, 0)
            act.wait_ge(wg_loaded, 16)
            nc.scalar.activation(w_g[0][:, :, :], wg_raw, ACT.Copy).then_inc(wg_hi, 1)
            act.wait_ge(m_done, 1)
            nc.scalar.activation(w_m[0][:, :, :], bank[0][:, :].rearrange("p (t c) -> p t c", t=T), ACT.Copy)\
                .then_inc(wm_hi, 1)
            ctx_high(0, 1)
            act.wait_ge(small_loaded, 16)
            nc.scalar.activation(tg[:, :], gates[:, :], ACT.Tanh).then_inc(tanh_done, 1)
            g_copy(0, 0)
            act.wait_ge(wp_loaded, 16)
            nc.scalar.activation(w_p[0][:, :, :], wp_raw, ACT.Copy).then_inc(wp_hi, 1)
            g_copy(0, 1)
            x_high(0, 0, early_xn[0])
            y_copy(0, 0)
            y_copy(0, 1)
            y_copy(0, 2)
            y_copy(0, 3)
            x_high(0, 1, early_xn[1])
            act.wait_ge(g_done, PAIRS)
            ctx_high(1, 0)
            ctx_high(1, 1)
            g_copy(0, 2)
            g_copy(0, 3)
            x_high(1, 0, early_xn[0])
            piece_high(0)
            x_high(1, 1, early_xn[1])
            g_copy(1, 0)
            g_copy(1, 1)
            piece_high(1)
            x1_center(0, 0)
            xt_high(0, 0)
            xt_high(0, 1)
            x1_center(0, 1)

            def step(i, prepare):
                for n in range(PAIRS):
                    g_copy(i, n)
                    if n in (1, 2):
                        xt_high(i - 1, 2 * n - 2)
                        xt_high(i - 1, 2 * n - 1)
                for n in range(PAIRS):
                    y_copy(i, n)
                    if n == 1 and prepare:
                        x_high(i + 1, 0, xn[:, :])
                if prepare:
                    ctx_high(i + 1, 0)
                    ctx_high(i + 1, 1)
                    x_high(i + 1, 1, xn[:, :])
                exps(i - 1, 0)
                exps(i - 1, 1)
                hct_high(i - 1, 0)
                x1_center(i, 0)
                finish(i - 1, 0)
                x1_center(i, 1)
                hct_high(i - 1, 1)
                if prepare:
                    finish(i - 1, 1)

            piece_high(2)
            g_copy(1, 2)
            xt_high(0, 2)
            xt_high(0, 3)
            piece_high(3)
            g_copy(1, 3)
            for n in range(PAIRS):
                y_copy(1, n)
            piece_high(4)
            piece_high(5)
            x_high(2, 0, xn[:, :])
            exps(0, 0)
            piece_high(6)
            x_high(2, 1, xn[:, :])
            hct_high(0, 0)
            exps(0, 1)
            ctx_high(2, 0)
            ctx_high(2, 1)
            finish(0, 0)
            x1_center(1, 0)
            hct_high(0, 1)
            x1_center(1, 1)
            finish(0, 1)
            with act.Fori(2, NB - 1) as i:
                step(i, True)
            step(NB - 1, False)
            xt_high(NB - 1, 0)
            xt_high(NB - 1, 1)
            finish(NB - 2, 1)
            xt_high(NB - 1, 2)
            xt_high(NB - 1, 3)
            exps(NB - 1, 0)
            exps(NB - 1, 1)
            hct_high(NB - 1, 0)
            finish(NB - 1, 0)
            hct_high(NB - 1, 1)
            finish_last()

        @block.vector
        def _(dve):
            xn_whole = xn[:, :]

            def x_stat(b, t):
                dve.wait_ge(x_loaded[t], count(16, b, 16))
                for h in range(HALVES):
                    last = nc.vector.bn_stats(x_stats[:, t, h, :], x_raw[:, t, h * NF:(h + 1) * NF])
                last.then_inc(x_stats_done, 1)

            def x_scalars(b, t):
                dve.wait_ge(x_stats_done, count(T, b, t + 1))
                nc.vector.memset(carrier[:, t:t + 1], 0.0)
                nc.vector.bn_aggr(x_mv[:, t, :], x_stats[:, t, :, :]).then_inc(x_mv_done, 1)
                dve.wait_ge(x_mv_done, count(T, b, t + 1))
                nc.vector.tensor_scalar(x_var[:, t:t + 1], x_mv[:, t, 1:2], EPS, None, ALU.add)\
                    .then_inc(x_var_ready, 1)

            def x_norm(b, t, normed):
                dve.wait_ge(x_rstd_ready, count(T, b, t + 1))
                if t == 0 and normed is xn_whole:
                    dve.wait_ge(att_part, count(PAIRS, b, 0))
                nc.vector.tensor_scalar(normed, x_raw[:, t, :], x_mv[:, t, 0:1], x_rstd[:, t:t + 1],
                                        ALU.subtract, ALU.mult).then_inc(xn_ready, 1)

            def x_low(b, t, normed):
                dve.wait_ge(x_hi_ready, count(T, b, t + 1))
                nc.vector.tensor_tensor(xs[1][:, t, :], normed, xs[0][:, t, :].bitcast(F32), ALU.subtract)\
                    .then_inc(x_lo_ready, 1)

            def sum_inputs(b, tiles=range(T)):
                for t in tiles:
                    dve.wait_ge(ctx_loaded[t], count(16, b, 16))
                    dve.wait_ge(x_loaded[t], count(16, b, 16))
                    nc.vector.scalar_tensor_tensor(w_sum[:, t, :], ctx_raw[:, t, :], tg[:, 0:1], x_raw[:, t, :],
                                                   ALU.mult, ALU.add).then_inc(w_sum_ready, 1)

            def att_sum(b, n):
                m, h = n // HALVES, n % HALVES
                dve.wait_ge(p_done, count(PAIRS, b, n + 1))
                dve.wait_ge(g_copied, count(PAIRS, b, n + 1))
                g = g_sb[:, n % 2, :]
                nc.vector.tensor_tensor_reduce(g, p_bank[n % 2][:, :], g, 1.0, 0.0, ALU.mult, ALU.add,
                                               row_sums[:, m, h:h + 1]).then_inc(att_part, 1)

            def y_stat(b, n):
                m, h = n // HALVES, n % HALVES
                dve.wait_ge(y_copied, count(PAIRS, b, n + 1))
                last = nc.vector.bn_stats(y_stats[:, m, h, :], y0[:, m, h * NF:(h + 1) * NF])
                if n == PAIRS - 1:
                    last.then_inc(y_chain, 1)

            def y_means(b):
                dve.wait_ge(y_chain, count(1, b, 1))
                nc.vector.memset(carrier[:, 2 * T:2 * T + 1], 0.0)
                for m in range(T):
                    last = nc.vector.bn_aggr(row_sums[:, m, 2:4], y_stats[:, m, :, :])
                last.then_inc(means_ready, 1)

            def group_means(b):
                def link(ins, k):
                    ins.then_inc(gn_chain, 1)
                    dve.wait_ge(gn_chain, count(6, b, k))
                sums = bank[0][:, 0:3 * T].rearrange("p (t k) -> p t k", t=T)
                dve.wait_ge(means_summed, count(1, b, 1))
                nc.vector.tensor_reduce(att[:, :], sums[:, :, 0:2], AX.X, ALU.add)
                link(nc.vector.tensor_scalar(g_mean[:, :], sums[:, :, 2], 1.0 / CG, None, ALU.mult), 1)
                nc.vector.tensor_tensor(att2[:, :], att[:, :], att[:, :], ALU.mult)
                link(nc.vector.tensor_tensor(dev[:, :], row_sums[:, :, 2], g_mean[:, :], ALU.subtract), 2)
                nc.vector.tensor_tensor(att_w[:, :], att[:, :], gn_tg[:, 0, :], ALU.mult)
                link(nc.vector.tensor_tensor(dev2[:, :], dev[:, :], dev[:, :], ALU.mult), 3)
                nc.vector.tensor_tensor(row_var[:, :], dev2[:, :], row_sums[:, :, 3], ALU.add)\
                    .then_inc(vars_ready, 1)

            def group_var(b):
                def link(ins, k):
                    ins.then_inc(gn_chain, 1)
                    dve.wait_ge(gn_chain, count(6, b, k))
                dve.wait_ge(vars_summed, count(1, b, 1))
                link(nc.vector.scalar_tensor_tensor(g_var[:, :], bank[0][:, 0:T], 1.0 / CG, att2[:, :],
                                                    ALU.mult, ALU.mult), 4)
                nc.vector.tensor_scalar(g_var_eps[:, :], g_var[:, :], EPS, None, ALU.add)\
                    .then_inc(g_var_ready, 1)

            def group_scalars(b):
                def link(ins, k):
                    ins.then_inc(gn_chain, 1)
                    dve.wait_ge(gn_chain, count(6, b, k))
                dve.wait_ge(g_rstd_ready, count(1, b, 1))
                link(nc.vector.tensor_tensor(gn_scale[:, :], att_w[:, :], g_rstd[:, :], ALU.mult), 5)
                link(nc.vector.tensor_tensor(gn_drop[:, :], gn_scale[:, :], g_mean[:, :], ALU.mult), 6)
                nc.vector.tensor_tensor(gn_shift[:, :], gn_tg[:, 1, :], gn_drop[:, :], ALU.subtract)

            def x1_sum(b, t):
                if t == 0:
                    dve.wait_ge(w_sum_ready, count(T, b, T))
                    if not opening(b):
                        dve.wait_ge(x1c_ready, count(T, b, 0))
                        dve.wait_ge(resid_ready, count(T, b, 0))
                nc.vector.scalar_tensor_tensor(x1[:, t, :], y0[:, t, :], gn_scale[:, t:t + 1],
                                               w_sum[:, t, :], ALU.mult, ALU.add).then_inc(x1_ready, 1)

            def x1_stat(b, t):
                dve.wait_ge(x1_ready, count(T, b, t + 1))
                for h in range(HALVES):
                    last = nc.vector.bn_stats(x1_stats[:, t, h, :], x1[:, t, h * NF:(h + 1) * NF])
                last.then_inc(x1_chain, 1)
                dve.wait_ge(x1_chain, count(2 * T, b, 2 * t + 1))
                nc.vector.memset(carrier[:, T + t:T + t + 1], 0.0)
                nc.vector.bn_aggr(x1_mv[:, t, :], x1_stats[:, t, :, :]).then_inc(x1_chain, 1)
                dve.wait_ge(x1_chain, count(2 * T, b, 2 * t + 2))
                nc.vector.tensor_scalar(x1_neg_mean[:, t:t + 1], x1_mv[:, t, 0:1], -1.0, None, ALU.mult)
                nc.vector.tensor_scalar(x1_var[:, t:t + 1], x1_mv[:, t, 1:2], EPS, None, ALU.add)\
                    .then_inc(x1_var_ready, 1)

            def xt_low(b, q):
                t, h = q // 2, q % 2
                at = (slice(None), slice(h * QB, (h + 1) * QB), slice(t * P, (t + 1) * P))
                dve.wait_ge(xt_hi_ready, count(NQ, b, q + 1))
                nc.vector.tensor_tensor(xt[1][at], xt_bank(b, q)[:, :].rearrange("p (k n) -> p k n", k=QB),
                                        xt[0][at].bitcast(F32), ALU.subtract).then_inc(xt_lo_ready, 1)

            def fin_scalars(b):
                dve.wait_ge(x1_rstd_ready, count(1, b, 1))
                dve.wait_ge(banks_read, banks_read_by(b - 1, T - 1))
                nc.vector.tensor_scalar(fin_scale[:, :], x1_rstd[:, :], tg[:, 1:2], None, ALU.mult)
                nc.vector.tensor_copy(fin_shift[:, :], gn_shift[:, :]).then_inc(fin_scalars_ready, 1)

            def gate(b, t):
                def link(ins, k):
                    ins.then_inc(gate_chain, 1)
                    dve.wait_ge(gate_chain, count(7 * T, b, 7 * t + k))
                dve.wait_ge(first_done, count(T, b, t + 1))
                link(nc.vector.tensor_scalar(logit[:, t, :], first_bank[t][:, ER:BASE], x1_rstd[:, t:t + 1],
                                             None, ALU.mult), 1)
                nc.vector.tensor_reduce(neg_max[:, t:t + 1], logit[:, t, :], AX.X, ALU.max, negate=True)\
                    .then_inc(gate_in_ready, 1)
                link(nc.vector.tensor_tensor(diff[:, t, :, :],
                                             logit[:, t, :].unsqueeze(1).broadcast_to((P, E, E)),
                                             logit[:, t, :].unsqueeze(2).broadcast_to((P, E, E)),
                                             ALU.subtract), 2)
                link(nc.vector.tensor_tensor(beats[:, t, :, :], diff[:, t, :, :], tie[:, :, :], ALU.is_ge), 3)
                link(nc.vector.tensor_reduce(rank[:, t, :], beats[:, t, :, :], AX.X, ALU.add), 4)
                dve.wait_ge(exp_done, count(T, b, t + 1))
                link(nc.vector.scalar_tensor_tensor(top[:, t, :], rank[:, t, :], TOP_K - 0.5, prob[:, t, :],
                                                    ALU.is_lt, ALU.mult, accum_out=top_sum[:, t:t + 1]), 5)
                link(nc.vector.reciprocal(top_inv[:, t:t + 1], top_sum[:, t:t + 1]), 6)
                link(nc.vector.tensor_scalar(combine[:, t, :], top[:, t, :], top_inv[:, t:t + 1], LORA_SCALE,
                                             ALU.mult, ALU.mult), 7)
                nc.vector.tensor_tensor(hc[:, t, :].rearrange("p (e r) -> p e r", e=E),
                                        first_bank[t][:, 0:ER].rearrange("p (e r) -> p e r", e=E),
                                        combine[:, t, :].unsqueeze(2).broadcast_to((P, E, R)),
                                        ALU.mult).then_inc(hc_ready, 1)

            def hct_low(b, t):
                dve.wait_ge(hct_hi_ready, count(T, b, t + 1))
                nc.vector.tensor_tensor(hct[1][:, t, :], tr_bank[1][:, 0:P], hct[0][:, t, :].bitcast(F32),
                                        ALU.subtract).then_inc(hct_lo_ready, 1)

            def ctx_low(b, t):
                dve.wait_ge(c_hi_ready, count(T, b, t + 1))
                nc.vector.tensor_tensor(cs[1][:, t, :], ctx_raw[:, t, :], cs[0][:, t, :].bitcast(F32),
                                        ALU.subtract).then_inc(c_lo_ready, 1)

            def piece_low(n):
                dve.wait_ge(piece_hi, n + 1)
                hi, lo = piece_parts(n)
                nc.vector.tensor_tensor(lo, piece_raw(n), hi.bitcast(F32), ALU.subtract)\
                    .then_inc(piece_split[n % 2], 1)

            nc.vector.memset(wz_diag[:, :, :], 0.0).then_inc(wz_cleared, 1)
            nc.vector.memset(group_ones[:, :], 0.0)
            nc.vector.memset(tie[:, :, :], TINY).then_inc(consts_filled, 1)
            nc.vector.memset(minus_half[:, :], -0.5).then_inc(consts_ready, 1)
            dve.wait_ge(consts_filled, 1)
            for q in range(P // CG):
                nc.vector.memset(group_ones[q * CG:(q + 1) * CG, q * CG:(q + 1) * CG], 1.0)
            for e in range(1, E):
                nc.vector.memset(tie[:, e, 0:e], 0.0)

            dve.wait_ge(wt_wz_loaded, 32)
            dve.wait_ge(wz_cleared, 1)
            for q in range(P // CG):
                rows = slice(q * CG, (q + 1) * CG)
                last = nc.vector.tensor_copy(wz_diag[rows, :, rows], wz_raw[rows, :, :])
            last.then_inc(wz_placed, 1)
            ctx_low(0, 0)
            dve.wait_ge(wm_hi, 1)
            nc.vector.tensor_tensor(w_m[1][:, :, :], bank[0][:, :].rearrange("p (t c) -> p t c", t=T),
                                    w_m[0][:, :, :].bitcast(F32), ALU.subtract).then_inc(wm_ready, 1)
            ctx_low(0, 1)
            dve.wait_ge(tanh_done, 1)
            for t in range(T):
                x_stat(0, t)
                x_scalars(0, t)
                sum_inputs(0, [t])
                x_norm(0, t, early_xn[t])
            x_stat(1, 0)
            x_low(0, 1, early_xn[1])
            x_scalars(1, 0)
            dve.wait_ge(gn_loaded, 16)
            nc.vector.tensor_scalar(gn_tg[:, :, :], gn_wb[:, :, :], tg[:, 0:1], None, ALU.mult)\
                .then_inc(gn_tg_ready, 1)
            y_stat(0, 0)
            y_stat(0, 1)
            att_sum(0, 0)
            dve.wait_ge(x_lo_ready, count(T, 1, 0))
            x_norm(1, 0, early_xn[0])
            att_sum(0, 1)
            y_stat(0, 2)
            att_sum(0, 2)
            y_stat(0, 3)
            x_stat(1, 1)
            x_scalars(1, 1)
            att_sum(0, 3)
            y_means(0)
            x_norm(1, 1, early_xn[1])
            dve.wait_ge(gn_tg_ready, 1)
            group_means(0)
            group_var(0)
            x_low(1, 1, early_xn[1])
            group_scalars(0)
            dve.wait_ge(x_lo_ready, count(T, 1, T))
            x1_sum(0, 0)
            x1_stat(0, 0)
            att_sum(1, 0)
            x1_sum(0, 1)
            x1_stat(0, 1)
            att_sum(1, 1)
            xt_low(0, 0)
            xt_low(0, 1)
            sum_inputs(1)

            def step(i, prepare):
                for n in range(PAIRS):
                    att_sum(i, n)
                    if n in (1, 2):
                        xt_low(i - 1, 2 * n - 2)
                        xt_low(i - 1, 2 * n - 1)
                        if prepare:
                            x_stat(i + 1, n - 1)
                if prepare:
                    for t in range(T):
                        x_scalars(i + 1, t)
                    x_norm(i + 1, 0, xn_whole)
                for n in range(PAIRS):
                    y_stat(i, n)
                y_means(i)
                if prepare:
                    x_low(i + 1, 0, xn_whole)
                    dve.wait_ge(x_lo_ready, count(T, i + 1, 1))
                    x_norm(i + 1, 1, xn_whole)
                fin_scalars(i - 1)
                gate(i - 1, 0)
                group_means(i)
                if prepare:
                    x_low(i + 1, 1, xn_whole)
                gate(i - 1, 1)
                group_var(i)
                group_scalars(i)
                x1_sum(i, 0)
                hct_low(i - 1, 0)
                x1_stat(i, 0)
                x1_sum(i, 1)
                x1_stat(i, 1)
                hct_low(i - 1, 1)
                if prepare:
                    sum_inputs(i + 1)

            att_sum(1, 2)
            xt_low(0, 2)
            xt_low(0, 3)
            att_sum(1, 3)
            piece_low(2)
            for n in range(PAIRS):
                y_stat(1, n)
            y_means(1)
            for t in range(T):
                x_stat(2, t)
            for t in range(T):
                x_scalars(2, t)
            piece_low(4)
            group_means(1)
            x_norm(2, 0, xn_whole)
            fin_scalars(0)
            gate(0, 0)
            dve.wait_ge(bias_loaded, 16)
            nc.vector.tensor_scalar(tf_bias[:, :], tf_bias[:, :], tg[:, 1:2], None, ALU.mult)\
                .then_inc(tf_bias_ready, 1)
            x_low(2, 0, xn_whole)
            dve.wait_ge(x_lo_ready, count(T, 2, 1))
            x_norm(2, 1, xn_whole)
            piece_low(6)
            group_var(1)
            hct_low(0, 0)
            gate(0, 1)
            x_low(2, 1, xn_whole)
            group_scalars(1)
            x1_sum(1, 0)
            x1_stat(1, 0)
            x1_sum(1, 1)
            hct_low(0, 1)
            x1_stat(1, 1)
            sum_inputs(2)
            with dve.Fori(2, NB - 1) as i:
                step(i, True)
            step(NB - 1, False)
            for q in range(NQ):
                xt_low(NB - 1, q)
            fin_scalars(NB - 1)
            gate(NB - 1, 0)
            gate(NB - 1, 1)
            hct_low(NB - 1, 0)
            hct_low(NB - 1, 1)
            dve.wait_ge(resid_ready, T * NB)
            for n, (lo, hi) in enumerate(CHUNKS):
                at = slice(max(lo - BASE, 0), hi - BASE)
                dve.wait_ge(tail_scaled, n + 1)
                nc.vector.tensor_tensor(fin[:, at], fin[:, at], resid[:, T - 1, at], ALU.add)\
                    .then_inc(tail_added, 1)

        @block.tensor
        def _(pe):
            def product(dst, weights, w_at, moving, m_at, steps, only=None):
                for k in range(steps) if only is None else [only]:
                    for a, c in PARTS:
                        last = nc.tensor.matmul(dst, w_at(weights[a], k), m_at(moving[c], k),
                                                start=(k == 0 and (a, c) == PARTS[0]),
                                                stop=(k == steps - 1 and (a, c) == PARTS[-1]))
                return last

            def chunk(weights, moving, dst, n, only=None):
                m, h = n // HALVES, n % HALVES
                return product(dst, weights, lambda w, k: w[:, k, m * P:(m + 1) * P],
                               moving, lambda v, k: v[:, k, h * NF:(h + 1) * NF], T, only)

            def p_chunk(b, n):
                chunk(w_p, xs, p_bank[n % 2][:, :], n).then_inc(p_done, 1)

            def g_chunk(b, n):
                chunk(w_g, cs, g_bank[n % 2][:, :], n).then_inc(g_done, 1)

            def pair(b, n):
                if n == 0:
                    pe.wait_ge(x_lo_ready, count(T, b, T))
                if n < 2:
                    pe.wait_ge(banks_read, banks_read_by(b - 2, n))
                else:
                    pe.wait_ge(att_part, count(PAIRS, b, n - 1))
                p_chunk(b, n)
                if n == 0:
                    pe.wait_ge(c_lo_ready, count(T, b, T))
                g_chunk(b, n)

            def transposes(b, groups):
                for q in groups:
                    t, h = q // 2, q % 2
                    if h == 0:
                        pe.wait_ge(x1c_ready, count(T, b, t + 1))
                    if q == 0:
                        pe.wait_ge(g_var_ready, count(1, b, 1))
                    elif q == 1:
                        pe.wait_ge(hct_lo_ready, credited(T, b, 0))
                    elif xt_bank(b, q) not in tr_bank:
                        pe.wait_ge(banks_read, banks_read_by(b - 1, 0))
                    else:
                        pe.wait_ge(xt_lo_ready, count(NQ, b, q - 1))
                    for j in range(QB):
                        k = h * QB + j
                        last = nc.tensor.transpose(xt_bank(b, q)[:, j * P:(j + 1) * P],
                                                   y0[:, t, k * P:(k + 1) * P], ident[:, :])
                    last.then_inc(xt_done, 1)

            def y_products(b):
                for n in range(PAIRS):
                    pe.wait_ge(att_part, count(PAIRS, b, 3 + n // 2))
                    chunk(w_m, cs, y_bank[n][:, :], n).then_inc(y_done, 1)

            def ffn_chunk(b, t, dst, n):
                lo, hi = CHUNKS[n]
                return product(dst, xt, lambda w, k: w[:, k, t * P:(t + 1) * P],
                               w_ext, lambda v, k: v[:, k, lo:hi], KD)

            def first_chunk(b, t):
                pe.wait_ge(xt_lo_ready, count(NQ, b, 2 * t + 2))
                pe.wait_ge(banks_read, banks_read_by(b - 1, t))
                if t == 0:
                    for split_done in piece_split:
                        pe.wait_ge(split_done, 1)
                ffn_chunk(b, t, first_bank[t][:, 0:CHUNKS[0][1]], 0).then_inc(first_done, 1)

            def sum_means(b, ffn):
                pe.wait_ge(means_ready, count(1, b, 1))
                if ffn:
                    pe.wait_ge(xt_lo_ready, count(NQ, b - 1, 3))
                nc.tensor.matmul(bank[0][:, 0:3 * T].rearrange("p (t k) -> p t k", t=T), group_ones[:, :],
                                 row_sums[:, :, 0:3], start=True, stop=True).then_inc(means_summed, 1)

            def sum_vars(b):
                pe.wait_ge(vars_ready, count(1, b, 1))
                nc.tensor.matmul(bank[0][:, 0:T], group_ones[:, :], row_var[:, :], start=True, stop=True)\
                    .then_inc(vars_summed, 1)

            def rest(b, t, attention):
                width = [hi - lo for lo, hi in CHUNKS]
                for n in range(2):
                    if attention:
                        pe.wait_ge(y_copied, count(PAIRS, b + 1, 2 * t + n + 1))
                    if t == 0:
                        for split_done in piece_split:
                            pe.wait_ge(split_done, n + 2)
                    ffn_chunk(b, t, rest_bank[t][n][:, 0:width[n + 1]], n + 1)
                    if n == 0:
                        pe.wait_ge(hc_ready, count(T, b, t + 1))
                        if t == 0:
                            pe.wait_ge(xt_lo_ready, count(NQ, b, NQ))
                        else:
                            pe.wait_ge(hct_lo_ready, credited(T, b, t))
                        nc.tensor.transpose(tr_bank[1][:, 0:P], hc[:, t, :], ident[:, :]).then_inc(hct_done, 1)
                if t == 0:
                    pe.wait_ge(piece_split[0], (PIECES + 1) // 2)
                pe.wait_ge(hct_lo_ready, credited(T, b, t + 1))
                dsts = [first_bank[t][:, BASE:width[0]], rest_bank[t][0][:, 0:width[1]],
                        rest_bank[t][1][:, 0:width[2]]]
                for n, ((lo, hi), dst) in enumerate(zip(CHUNKS, dsts)):
                    for a, c in PARTS:
                        last = nc.tensor.matmul(dst, hct[a][:, t, :], b_up[c][:, max(lo - BASE, 0):hi - BASE],
                                                start=False, stop=True, skip_group_check=True)
                    if not attention and t == T - 1 and n < 2:
                        last.then_inc(tail_done, 1)
                last.then_inc(ffn_done, 1)

            pe.wait_ge(wz_placed, 1)
            for m in range(T):
                for k in range(T):
                    last = nc.tensor.matmul(bank[0][:, m * C + k * P:m * C + (k + 1) * P],
                                            wt_raw[:, k, m * P:(m + 1) * P], wz_diag[:, k, :],
                                            start=True, stop=True)
            last.then_inc(m_done, 1)
            pe.wait_ge(wg_ready, 1)
            for k in range(T):
                pe.wait_ge(c_lo_ready, k + 1)
                for n in range(2):
                    last = chunk(w_g, cs, g_bank[n][:, :], n, only=k)
                    if k == T - 1:
                        last.then_inc(g_done, 1)
                if k == 0:
                    pe.wait_ge(wm_ready, 1)
                    for n in (0, 2):
                        chunk(w_m, cs, y_bank[n][:, :], n, only=0)
            for n in range(PAIRS):
                if n % 2:
                    pe.wait_ge(g_copied, n // 2 + 1)
                chunk(w_m, cs, y_bank[n][:, :], n, only=None if n % 2 else 1).then_inc(y_done, 1)
            for n in range(2, PAIRS):
                pe.wait_ge(y_copied, 2 * n - 2)
                g_chunk(0, n)
            pe.wait_ge(wp_ready, 1)
            pe.wait_ge(x_lo_ready, T)
            for n in range(PAIRS):
                if n < 2:
                    pe.wait_ge(y_copied, 2 * n + 1)
                else:
                    pe.wait_ge(att_part, n - 1)
                p_chunk(0, n)
            pe.wait_ge(c_lo_ready, count(T, 1, T))
            pe.wait_ge(g_copied, 3)
            g_chunk(1, 0)
            sum_means(0, False)
            pe.wait_ge(g_copied, 4)
            g_chunk(1, 1)
            sum_vars(0)
            pe.wait_ge(x_lo_ready, count(T, 1, T))
            for n in range(2):
                pe.wait_ge(att_part, 3 + n)
                p_chunk(1, n)
            pe.wait_ge(ident_ready, 1)

            def step(i, prepare):
                transposes(i - 1, (0, 1))
                pair(i, 2)
                transposes(i - 1, (2, 3))
                pair(i, 3)
                y_products(i)
                first_chunk(i - 1, 0)
                sum_means(i, True)
                first_chunk(i - 1, 1)
                sum_vars(i)
                rest(i - 1, 0, True)
                rest(i - 1, 1, True)
                if prepare:
                    pair(i + 1, 0)
                    pair(i + 1, 1)

            with pe.Fori(1, NB - 1) as i:
                step(i, True)
            step(NB - 1, False)
            transposes(NB - 1, range(NQ))
            first_chunk(NB - 1, 0)
            first_chunk(NB - 1, 1)
            rest(NB - 1, 0, False)
            rest(NB - 1, 1, False)


_OUT_SHAPE = (8, 256, 1024)


def kernel(x, ctx_4096, g_xattn, g_ffn, L0_xattn_Wt, L0_xattn_Wp, L0_xattn_Wg, L0_xattn_Wz, L0_xattn_gn_w,
           L0_xattn_gn_b, L0_ffn_W_base, L0_ffn_b_base, L0_ffn_W_router, L0_ffn_A_stack, L0_ffn_B_stack):
    import numpy as np
    import concourse.bacc as bacc
    from concourse.bass_utils import run_bass_kernel_spmd

    groups = 8
    cg = L0_xattn_Wz.shape[1]
    experts, rank, d = L0_ffn_A_stack.shape
    a_rows = np.asarray(L0_ffn_A_stack).reshape(experts * rank, d)
    w_rows = np.concatenate([a_rows, np.asarray(L0_ffn_W_router), np.asarray(L0_ffn_W_base)], axis=0)
    arrays = {
        "x": x, "ctx": ctx_4096, "g_both": np.concatenate([g_xattn, g_ffn]),
        "wt": L0_xattn_Wt, "wp_t": np.asarray(L0_xattn_Wp).T, "wg_t": np.asarray(L0_xattn_Wg).T,
        "wz_t": np.asarray(L0_xattn_Wz).reshape(groups, cg, cg).transpose(0, 2, 1),
        "gn_cols": np.stack([L0_xattn_gn_w, L0_xattn_gn_b]).reshape(2, -1, P).transpose(2, 0, 1),
        "w_ext_t": w_rows.T, "b_base": L0_ffn_b_base,
        "b_stack_t": np.asarray(L0_ffn_B_stack).transpose(0, 2, 1).reshape(experts * rank, -1),
    }
    nc = bacc.Bacc("TRN2", target_bir_lowering=False, num_devices=1)
    feeds, args = {}, []
    for name, a in arrays.items():
        a = np.ascontiguousarray(a)
        feeds[f"in_{name}"] = a
        args.append(nc.dram_tensor(f"in_{name}", a.shape, mybir.dt.from_np(a.dtype), kind="ExternalInput").ap())
    out = nc.dram_tensor("out", _OUT_SHAPE, F32, kind="ExternalOutput").ap()
    gated_block_kernel(nc, *args, out)
    r = run_bass_kernel_spmd(nc, [feeds], core_ids=[0])
    return r.results[0]["out"]
```
